# Optimizing a Trainium2 kernel written in Bass

```python
import numpy as np
import jax
import jax.numpy as jnp

def _softmax(x, axis=-1):
    return jax.nn.softmax(x, axis=axis)
def _gelu(x):
    return jax.nn.gelu(x, approximate=True)
def _silu(x):
    return jax.nn.silu(x)
def _sigmoid(x):
    return jax.nn.sigmoid(x)
def _layernorm(x, axis=-1, eps=1e-5):
    m = jnp.mean(x, axis=axis, keepdims=True)
    v = jnp.var(x, axis=axis, keepdims=True)
    return (x - m) / jnp.sqrt(v + eps)
def _scatter_add(tgt, idx, src, axis=0):
    return tgt.at[idx].add(src)
def _segment_sum(src, seg, n):
    return jax.ops.segment_sum(src, seg, n)

kernel_name = 'mk_conv_seq_d4_conv_nchw128_73e15d'

def setup_inputs(seed: int = 0):
    np.random.seed(seed)
    _w = jnp.asarray
    def _rec_inputs():
        import jax
        import jax.numpy as jnp
        _gk = jax.random.key(seed)
        x = -0.0005207 + 1.001 * jax.random.normal(jax.random.fold_in(_gk, 1), (4, 128, 64, 64), jnp.float32)
        return x
    x = _rec_inputs()
    def _L0_conv_setup():
        import jax, jax.numpy as jnp
        import numpy as np
        GROUPS = 8
        NUM_HEADS = 4
        EPS = 1e-05

        def group_norm(x, w, b):
            B, C, H, W = x.shape
            xg = x.reshape(B, GROUPS, C // GROUPS, H, W)
            mean = jnp.mean(xg, axis=(2, 3, 4), keepdims=True)
            var = jnp.var(xg, axis=(2, 3, 4), keepdims=True)
            xn = ((xg - mean) * jax.lax.rsqrt(var + EPS)).reshape(B, C, H, W)
            return xn * w[None, :, None, None] + b[None, :, None, None]
        key = jax.random.key(seed)
        k1, k2, k3 = jax.random.split(key, 3)
        B, C, H, W = (4, 128, 64, 64)
        x = jax.random.normal(k1, (B, C, H, W), dtype=jnp.float32)
        gn_w = jnp.ones((C,), jnp.float32)
        gn_b = jnp.zeros((C,), jnp.float32)
        qkv_w = jax.random.normal(k2, (3 * C, C), dtype=jnp.float32) * (1.0 / np.sqrt(C))
        qkv_b = jnp.zeros((3 * C,), jnp.float32)
        proj_w = jax.random.normal(k3, (C, C), dtype=jnp.float32) * (1.0 / np.sqrt(C))
        proj_b = jnp.zeros((C,), jnp.float32)
        return {'x': x, 'gn_w': gn_w, 'gn_b': gn_b, 'qkv_w': qkv_w, 'qkv_b': qkv_b, 'proj_w': proj_w, 'proj_b': proj_b}
    _L0_conv_all = _L0_conv_setup()
    _L0_conv_in = {k: v for k, v in _L0_conv_all.items() if k in ('gn_w', 'gn_b', 'qkv_w', 'qkv_b', 'proj_w', 'proj_b', )}
    del _L0_conv_all

    def _L1_conv_setup():
        import jax, jax.numpy as jnp
        import numpy as np
        EPS = 1e-05

        def _binary_act(x):
            out3 = jnp.where(x < -1, -1.0, jnp.where(x < 0, x * x + 2.0 * x, jnp.where(x < 1, -x * x + 2.0 * x, 1.0)))
            return jax.lax.stop_gradient(jnp.sign(x) - out3) + out3

        def _binarize_weights(w):
            scale = jax.lax.stop_gradient(jnp.mean(jnp.abs(w), axis=(1, 2, 3), keepdims=True))
            clipped = jnp.clip(w, -1.0, 1.0)
            return jax.lax.stop_gradient(scale * jnp.sign(w) - clipped) + clipped
        key = jax.random.key(seed)
        kx, kw = jax.random.split(key)
        B, Cin, Cout, H, W = (32, 128, 128, 56, 56)
        x = jax.random.normal(kx, (B, Cin, H, W), dtype=jnp.float32)
        w = jax.random.uniform(kw, (Cout, Cin, 3, 3), dtype=jnp.float32) * 0.001
        return {'x': x, 'bias0': jnp.zeros((Cin,), jnp.float32), 'w': w, 'gamma': jnp.ones((Cout,), jnp.float32), 'beta': jnp.zeros((Cout,), jnp.float32), 'bias1': jnp.zeros((Cout,), jnp.float32), 'alpha': jnp.full((Cout,), 0.25, jnp.float32), 'bias2': jnp.zeros((Cout,), jnp.float32)}
    _L1_conv_all = _L1_conv_setup()
    _L1_conv_in = {k: v for k, v in _L1_conv_all.items() if k in ('bias0', 'w', 'gamma', 'beta', 'bias1', 'alpha', 'bias2', )}
    del _L1_conv_all

    def _L2_conv_setup():
        import jax, jax.numpy as jnp
        import numpy as np
        WS = 8
        K = 4
        key = jax.random.key(seed)
        ks = jax.random.split(key, 8)
        B, C, H, W = (4, 128, 128, 128)
        d_in, d_state, dt_rank = (256, 16, 8)
        A_init = jnp.tile(jnp.arange(1, d_state + 1, dtype=jnp.float32), (d_in, 1))
        return {'x': jax.random.normal(ks[0], (B, C, H, W), jnp.float32), 'ln_g': jnp.ones((C,), jnp.float32), 'ln_b': jnp.zeros((C,), jnp.float32), 'W_in': jax.random.normal(ks[1], (C, 2 * d_in), jnp.float32) * C ** (-0.5), 'b_in': jnp.zeros((2 * d_in,), jnp.float32), 'conv_w': jax.random.normal(ks[2], (d_in, K), jnp.float32) * 0.3, 'conv_b': jnp.zeros((d_in,), jnp.float32), 'W_x': jax.random.normal(ks[3], (d_in, dt_rank + 2 * d_state), jnp.float32) * d_in ** (-0.5), 'dt_w': jax.random.normal(ks[4], (dt_rank, d_in), jnp.float32) * dt_rank ** (-0.5), 'dt_b': jnp.full((d_in,), -4.0, jnp.float32), 'A_log': jnp.log(A_init), 'D': jnp.ones((d_in,), jnp.float32), 'W_out': jax.random.normal(ks[5], (d_in, C), jnp.float32) * d_in ** (-0.5), 'b_out': jnp.zeros((C,), jnp.float32)}
    _L2_conv_all = _L2_conv_setup()
    _L2_conv_in = {k: v for k, v in _L2_conv_all.items() if k in ('ln_g', 'ln_b', 'W_in', 'b_in', 'conv_w', 'conv_b', 'W_x', 'dt_w', 'dt_b', 'A_log', 'D', 'W_out', 'b_out', )}
    del _L2_conv_all

    def _L3_conv_setup():
        import jax, jax.numpy as jnp
        import numpy as np
        MIDC = 128
        HEADS = 8
        HEADC = MIDC // HEADS
        EPS = 1e-05

        def _ln(t, w, b):
            m = t.mean(-1, keepdims=True)
            s = jnp.std(t, axis=-1, ddof=1, keepdims=True)
            return w * ((t - m) / (s + EPS)) + b
        key = jax.random.key(seed)
        ks = jax.random.split(key, 8)
        B, C, H, W = (8, MIDC, 256, 256)
        s = 1.0 / np.sqrt(C)
        x = jax.random.normal(ks[0], (B, C, H, W), dtype=jnp.float32)
        qkv_w = jax.random.normal(ks[1], (3 * C, C), dtype=jnp.float32) * s
        o1_w = jax.random.normal(ks[2], (C, C), dtype=jnp.float32) * s
        o2_w = jax.random.normal(ks[3], (C, C), dtype=jnp.float32) * s
        kln_w = 1.0 + 0.1 * jax.random.normal(ks[4], (HEADS, 1, HEADC), dtype=jnp.float32)
        kln_b = 0.1 * jax.random.normal(ks[5], (HEADS, 1, HEADC), dtype=jnp.float32)
        vln_w = 1.0 + 0.1 * jax.random.normal(ks[6], (HEADS, 1, HEADC), dtype=jnp.float32)
        vln_b = 0.1 * jax.random.normal(ks[7], (HEADS, 1, HEADC), dtype=jnp.float32)
        return {'x': x, 'qkv_w': qkv_w, 'o1_w': o1_w, 'o2_w': o2_w, 'kln_w': kln_w, 'kln_b': kln_b, 'vln_w': vln_w, 'vln_b': vln_b}
    _L3_conv_all = _L3_conv_setup()
    _L3_conv_in = {k: v for k, v in _L3_conv_all.items() if k in ('qkv_w', 'o1_w', 'o2_w', 'kln_w', 'kln_b', 'vln_w', 'vln_b', )}
    del _L3_conv_all

    return {
        "x": x,
        "L0_conv_gn_w": _L0_conv_in["gn_w"],
        "L0_conv_gn_b": _L0_conv_in["gn_b"],
        "L0_conv_qkv_w": _L0_conv_in["qkv_w"],
        "L0_conv_qkv_b": _L0_conv_in["qkv_b"],
        "L0_conv_proj_w": _L0_conv_in["proj_w"],
        "L0_conv_proj_b": _L0_conv_in["proj_b"],
        "L1_conv_bias0": _L1_conv_in["bias0"],
        "L1_conv_w": _L1_conv_in["w"],
        "L1_conv_gamma": _L1_conv_in["gamma"],
        "L1_conv_beta": _L1_conv_in["beta"],
        "L1_conv_bias1": _L1_conv_in["bias1"],
        "L1_conv_alpha": _L1_conv_in["alpha"],
        "L1_conv_bias2": _L1_conv_in["bias2"],
        "L2_conv_ln_g": _L2_conv_in["ln_g"],
        "L2_conv_ln_b": _L2_conv_in["ln_b"],
        "L2_conv_W_in": _L2_conv_in["W_in"],
        "L2_conv_b_in": _L2_conv_in["b_in"],
        "L2_conv_conv_w": _L2_conv_in["conv_w"],
        "L2_conv_conv_b": _L2_conv_in["conv_b"],
        "L2_conv_W_x": _L2_conv_in["W_x"],
        "L2_conv_dt_w": _L2_conv_in["dt_w"],
        "L2_conv_dt_b": _L2_conv_in["dt_b"],
        "L2_conv_A_log": _L2_conv_in["A_log"],
        "L2_conv_D": _L2_conv_in["D"],
        "L2_conv_W_out": _L2_conv_in["W_out"],
        "L2_conv_b_out": _L2_conv_in["b_out"],
        "L3_conv_qkv_w": _L3_conv_in["qkv_w"],
        "L3_conv_o1_w": _L3_conv_in["o1_w"],
        "L3_conv_o2_w": _L3_conv_in["o2_w"],
        "L3_conv_kln_w": _L3_conv_in["kln_w"],
        "L3_conv_kln_b": _L3_conv_in["kln_b"],
        "L3_conv_vln_w": _L3_conv_in["vln_w"],
        "L3_conv_vln_b": _L3_conv_in["vln_b"],
    }

def reference(x, L0_conv_gn_w, L0_conv_gn_b, L0_conv_qkv_w, L0_conv_qkv_b, L0_conv_proj_w, L0_conv_proj_b, L1_conv_bias0, L1_conv_w, L1_conv_gamma, L1_conv_beta, L1_conv_bias1, L1_conv_alpha, L1_conv_bias2, L2_conv_ln_g, L2_conv_ln_b, L2_conv_W_in, L2_conv_b_in, L2_conv_conv_w, L2_conv_conv_b, L2_conv_W_x, L2_conv_dt_w, L2_conv_dt_b, L2_conv_A_log, L2_conv_D, L2_conv_W_out, L2_conv_b_out, L3_conv_qkv_w, L3_conv_o1_w, L3_conv_o2_w, L3_conv_kln_w, L3_conv_kln_b, L3_conv_vln_w, L3_conv_vln_b):
    import jax
    import jax.numpy as jnp
    def _L0_conv_ref(x, gn_w, gn_b, qkv_w, qkv_b, proj_w, proj_b):
        import jax, jax.numpy as jnp
        import numpy as np
        GROUPS = 8
        NUM_HEADS = 4
        EPS = 1e-05

        def group_norm(x, w, b):
            B, C, H, W = x.shape
            xg = x.reshape(B, GROUPS, C // GROUPS, H, W)
            mean = jnp.mean(xg, axis=(2, 3, 4), keepdims=True)
            var = jnp.var(xg, axis=(2, 3, 4), keepdims=True)
            xn = ((xg - mean) * jax.lax.rsqrt(var + EPS)).reshape(B, C, H, W)
            return xn * w[None, :, None, None] + b[None, :, None, None]
        B, C, H, W = x.shape
        nh = NUM_HEADS
        hd = C // nh
        xn = group_norm(x, gn_w, gn_b)
        qkv = jnp.einsum('oc,bchw->bohw', qkv_w, xn) + qkv_b[None, :, None, None]
        qkv = qkv.reshape(B, 3, nh, hd, H * W)
        q, k, v = (qkv[:, 0], qkv[:, 1], qkv[:, 2])
        attn = jnp.einsum('bhcd,bhce->bhde', q, k) * C ** (-0.5)
        attn = jax.nn.softmax(attn, axis=-1)
        out = jnp.einsum('bhde,bhce->bhcd', attn, v).reshape(B, C, H, W)
        out = jnp.einsum('oc,bchw->bohw', proj_w, out) + proj_b[None, :, None, None]
        return out + xn

    def _L1_conv_ref(x, bias0, w, gamma, beta, bias1, alpha, bias2):
        import jax, jax.numpy as jnp
        import numpy as np
        EPS = 1e-05

        def _binary_act(x):
            out3 = jnp.where(x < -1, -1.0, jnp.where(x < 0, x * x + 2.0 * x, jnp.where(x < 1, -x * x + 2.0 * x, 1.0)))
            return jax.lax.stop_gradient(jnp.sign(x) - out3) + out3

        def _binarize_weights(w):
            scale = jax.lax.stop_gradient(jnp.mean(jnp.abs(w), axis=(1, 2, 3), keepdims=True))
            clipped = jnp.clip(w, -1.0, 1.0)
            return jax.lax.stop_gradient(scale * jnp.sign(w) - clipped) + clipped
        def pc(v):
            return v[None, :, None, None]
        residual = x
        out = x + pc(bias0)
        out = _binary_act(out)
        bw = _binarize_weights(w)
        y = jax.lax.conv_general_dilated(out, bw, window_strides=(1, 1), padding=((1, 1), (1, 1)), dimension_numbers=('NCHW', 'OIHW', 'NCHW'))
        mean = jnp.mean(y, axis=(0, 2, 3), keepdims=True)
        var = jnp.mean(jnp.square(y - mean), axis=(0, 2, 3), keepdims=True)
        y = (y - mean) * jax.lax.rsqrt(var + EPS) * pc(gamma) + pc(beta)
        y = y + residual
        y = y + pc(bias1)
        y = jnp.where(y >= 0, y, pc(alpha) * y)
        y = y + pc(bias2)
        return y

    def _L2_conv_ref(x, ln_g, ln_b, W_in, b_in, conv_w, conv_b, W_x, dt_w, dt_b, A_log, D, W_out, b_out):
        import jax, jax.numpy as jnp
        import numpy as np
        WS = 8
        K = 4
        B, C, H, W = x.shape
        nh, nw = (H // WS, W // WS)
        L = WS * WS
        d_in = W_in.shape[1] // 2
        dt_rank = dt_w.shape[0]
        d_state = A_log.shape[1]
        t = x.reshape(B, C, nh, WS, nw, WS).transpose(0, 2, 4, 3, 5, 1).reshape(-1, L, C)
        mu = t.mean(-1, keepdims=True)
        var = t.var(-1, keepdims=True)
        tn = (t - mu) * jax.lax.rsqrt(var + 1e-05) * ln_g + ln_b
        xz = tn @ W_in + b_in
        xi, z = (xz[..., :d_in], xz[..., d_in:])
        xp = jnp.pad(xi, ((0, 0), (K - 1, 0), (0, 0)))
        xc = sum((xp[:, k:k + L, :] * conv_w[:, k] for k in range(K))) + conv_b
        xc = jax.nn.silu(xc)
        dbl = xc @ W_x
        dr = dbl[..., :dt_rank]
        Bm = dbl[..., dt_rank:dt_rank + d_state]
        Cm = dbl[..., dt_rank + d_state:]
        delta = jax.nn.softplus(dr @ dt_w + dt_b)
        A = -jnp.exp(A_log)

        def step(h, inputs):
            d_t, B_t, C_t, x_t = inputs
            dA = jnp.exp(d_t[:, :, None] * A)
            h = dA * h + (d_t * x_t)[:, :, None] * B_t[:, None, :]
            y = jnp.einsum('nds,ns->nd', h, C_t)
            return (h, y)
        n = xc.shape[0]
        h0 = jnp.zeros((n, d_in, d_state), xc.dtype)
        xs = (delta.transpose(1, 0, 2), Bm.transpose(1, 0, 2), Cm.transpose(1, 0, 2), xc.transpose(1, 0, 2))
        _, ys = jax.lax.scan(step, h0, xs)
        y = ys.transpose(1, 0, 2) + xc * D
        y = y * jax.nn.silu(z)
        out = y @ W_out + b_out
        out = out.reshape(B, nh, nw, WS, WS, C).transpose(0, 5, 1, 3, 2, 4).reshape(B, C, H, W)
        return out + x

    def _L3_conv_ref(x, qkv_w, o1_w, o2_w, kln_w, kln_b, vln_w, vln_b):
        import jax, jax.numpy as jnp
        import numpy as np
        MIDC = 128
        HEADS = 8
        HEADC = MIDC // HEADS
        EPS = 1e-05

        def _ln(t, w, b):
            m = t.mean(-1, keepdims=True)
            s = jnp.std(t, axis=-1, ddof=1, keepdims=True)
            return w * ((t - m) / (s + EPS)) + b
        B, C, H, W = x.shape
        hc = C // HEADS
        N = H * W
        qkv = jnp.einsum('oc,bchw->bhwo', qkv_w, x)
        qkv = qkv.reshape(B, N, HEADS, 3 * hc).transpose(0, 2, 1, 3)
        q, k, v = jnp.split(qkv, 3, axis=-1)
        k = _ln(k, kln_w, kln_b)
        v = _ln(v, vln_w, vln_b)
        kv = jnp.einsum('bhnd,bhne->bhde', k, v) / N
        o = jnp.einsum('bhnd,bhde->bhne', q, kv)
        o = o.transpose(0, 2, 1, 3).reshape(B, H, W, C).transpose(0, 3, 1, 2)
        ret = o + x
        u = jnp.einsum('oc,bchw->bohw', o1_w, ret)
        u = jax.nn.gelu(u, approximate=False)
        u = jnp.einsum('oc,bchw->bohw', o2_w, u) + x
        return jax.nn.gelu(u, approximate=False)

    def _gn(v, G=32, eps=1e-5):
        B_, C_, H_, W_ = v.shape
        g = v.reshape(B_, G, C_ // G, H_, W_)
        m = jnp.mean(g, axis=(2, 3, 4), keepdims=True)
        s = jnp.var(g, axis=(2, 3, 4), keepdims=True)
        return ((g - m) / jnp.sqrt(s + eps)).reshape(v.shape)

    def _ln_c(v, eps=1e-6):
        m = jnp.mean(v, axis=1, keepdims=True)
        s = jnp.var(v, axis=1, keepdims=True)
        return (v - m) / jnp.sqrt(s + eps)

    def _ln_t(v, eps=1e-5):
        m = jnp.mean(v, axis=-1, keepdims=True)
        s = jnp.var(v, axis=-1, keepdims=True)
        return (v - m) / jnp.sqrt(s + eps)

    def _to_tokens(v):
        B_, C_, H_, W_ = v.shape
        return v.reshape(B_, C_, H_ * W_).transpose(0, 2, 1)
    def _from_tokens(t, like):
        B_, C_, H_, W_ = like.shape
        return t.transpose(0, 2, 1).reshape(B_, C_, H_, W_)

    x = _L0_conv_ref(x, L0_conv_gn_w, L0_conv_gn_b, L0_conv_qkv_w, L0_conv_qkv_b, L0_conv_proj_w, L0_conv_proj_b)
    x = _L1_conv_ref(x, L1_conv_bias0, L1_conv_w, L1_conv_gamma, L1_conv_beta, L1_conv_bias1, L1_conv_alpha, L1_conv_bias2)
    x = _L2_conv_ref(x, L2_conv_ln_g, L2_conv_ln_b, L2_conv_W_in, L2_conv_b_in, L2_conv_conv_w, L2_conv_conv_b, L2_conv_W_x, L2_conv_dt_w, L2_conv_dt_b, L2_conv_A_log, L2_conv_D, L2_conv_W_out, L2_conv_b_out)
    x = _L3_conv_ref(x, L3_conv_qkv_w, L3_conv_o1_w, L3_conv_o2_w, L3_conv_kln_w, L3_conv_kln_b, L3_conv_vln_w, L3_conv_vln_b)
    return x


_drawn_inputs = setup_inputs


def setup_inputs(seed=0):
    import zlib

    import numpy as np

    out = dict(_drawn_inputs(seed))
    spreads = {'L0_conv_gn_w': (1.0, 0.2),
     'L0_conv_gn_b': (0.0, 0.1),
     'L0_conv_qkv_b': (0.0, 0.1),
     'L0_conv_proj_b': (0.0, 0.1),
     'L1_conv_bias0': (0.0, 0.1),
     'L1_conv_gamma': (1.0, 0.2),
     'L1_conv_beta': (0.0, 0.1),
     'L1_conv_bias1': (0.0, 0.1),
     'L1_conv_alpha': (0.25, 0.2),
     'L1_conv_bias2': (0.0, 0.1),
     'L2_conv_ln_g': (1.0, 0.2),
     'L2_conv_ln_b': (0.0, 0.289),
     'L2_conv_b_in': (0.0, 0.276),
     'L2_conv_conv_b': (0.0, 0.1),
     'L2_conv_dt_b': (-4.0, 0.6),
     'L2_conv_D': (1.0, 0.6),
     'L2_conv_b_out': (0.0, 2.0)}
    factors = {'L1_conv_w': 200.0, 'L2_conv_W_x': 6.4, 'L2_conv_dt_w': 8.0, 'L2_conv_A_log': 8.0}
    for name, (base, spread) in spreads.items():
        noise = np.random.default_rng([zlib.crc32(name.encode()), seed]).standard_normal(out[name].shape)
        drawn = base * np.exp(spread * noise) if base else spread * noise
        out[name] = jnp.asarray(drawn.astype(out[name].dtype))
    for name, factor in factors.items():
        out[name] = (out[name] * factor).astype(out[name].dtype)
    return out
```

```python
from contextlib import ExitStack, contextmanager

import concourse.bass as bass
from concourse import mybir

F32 = mybir.dt.float32
F16 = mybir.dt.float16
BF16 = mybir.dt.bfloat16
ALU = mybir.AluOpType
ACT = mybir.ActivationFunctionType
AX = mybir.AxisListType

B, C, H, W = 4, 128, 64, 64
HW = H * W
N = B * HW
CH = 512
CPB = HW // CH


class Tally:

    def __init__(self, primed=0):
        self.n = primed
        self.loops = []

    def value(self, ahead=0):
        v = self.n + ahead
        for term in self.loops:
            v = term + v
        return v

    def next(self, ahead=0):
        self.n += 1
        return self.value(ahead)


@contextmanager
def counted_loop(eng, count, *tallies):
    before = [t.n for t, _ in tallies]
    with eng.Fori(0, count) as i:
        for t, k in tallies:
            t.loops.append(i * k)
        yield i
        for (t, k), n in zip(tallies, before):
            assert t.n - n == k, (t.n - n, k)
    for (t, k), n in zip(tallies, before):
        t.loops.pop()
        t.n = n + count * k


class Chain:

    def __init__(self, eng, sem):
        self.eng, self.sem, self.done = eng, sem, Tally()

    def step(self, ins):
        ins.then_inc(self.sem, 1)
        self.eng.wait_ge(self.sem, self.done.next())
GROUPS = 8
HEADS = 4
HD = C // HEADS
ET = HW // 128
PAIRS = ET // 2
DT = CH // 128
ABLK = DT * CPB
QBOUND = 4096.0
MROW = 32768.0


def setup_attention(nc, d, X, t):
    with ExitStack() as ctx:
        sem = lambda n: ctx.enter_context(nc.semaphore(n))
        sb = lambda n, s, dt=F32: ctx.enter_context(nc.sbuf_tensor(n, s, dt))
        ps = ctx.enter_context(nc.psum_tensor("setup_ps", [128, 512], F32))
        x_in = [sem(f"x_in{b}") for b in range(B)]
        const_in, dve_step, pe_step, act_step = sem("const_in"), sem("su_dve"), sem("su_pe"), sem("su_act")
        stats = sb("gn_stats", [128, B, CPB, 6])
        cst = sb("gn_channel", [128, B, 2])
        grp = sb("gn_group", [128, 8, B])
        vec = sb("l0_vec", [128, 8])
        group_avg = sb("group_avg", [128, 128])
        ones_row = sb("ones_row", [1, 128])
        absw = sb("absw", [128, 256])
        bnd = sb("bnd", [128, 4])
        row = sb("bnd_row", [1, 256])
        top = sb("bnd_top", [1, 2])
        block = ctx.enter_context(nc.Block())
        loads = [(t.qk_w, d["qk_w"]), (t.v_w, d["v_w"]), (t.proj_w, d["proj_w"]), (vec, d["l0_vec"]),
                 (t.qk_b, d["qk_b"]), (group_avg, d["group_avg"]), (ones_row, d["ones_row"]), (t.ident, d["ident"]),
                 (t.sel, d["sel"]), (t.qk_full, d["qk_full"])]

        @block.sync
        def _(sp):
            for b in range(B):
                sp.dma_start(X[:, b * HW:(b + 1) * HW], d["x"][:, b, :]).then_inc(x_in[b], 16)

        @block.scalar
        def _(act):
            for dst, src in loads:
                act.dma_start(dst[:], src).then_inc(const_in, 16)
            act.wait_ge(dve_step, V_VAR)
            nc.scalar.activation(grp[:, 5, :], grp[:, 4, :], ACT.Sqrt).then_inc(act_step, 1)

        @block.vector
        def _(dve):
            ch = Chain(dve, dve_step)
            for b in range(B):
                dve.wait_ge(x_in[b], 16)
                for k in range(CPB):
                    nc.vector.bn_stats(stats[:, b, k, :], X[:, b * HW + k * CH: b * HW + (k + 1) * CH]).then_inc(dve_step, 1)
                    ch.done.n += 1
                dve.wait_ge(dve_step, ch.done.value())
                ch.step(nc.vector.bn_aggr(cst[:, b, :], stats[:, b, :, :].rearrange("p k s -> p (k s)")))
            assert ch.done.n == V_STAT, ch.done.n
            dve.wait_ge(const_in, 16 * len(loads))
            dve.wait_ge(pe_step, 1)
            ch.step(nc.vector.tensor_copy(grp[:, 0, :], ps[:, 0:B]))
            ch.step(nc.vector.tensor_tensor(grp[:, 1, :], cst[:, :, 0], grp[:, 0, :], ALU.subtract))
            ch.step(nc.vector.tensor_tensor(grp[:, 2, :], grp[:, 1, :], grp[:, 1, :], ALU.mult))
            ch.step(nc.vector.tensor_tensor(grp[:, 3, :], grp[:, 2, :], cst[:, :, 1], ALU.add))
            assert ch.done.n == V_DEV, ch.done.n
            dve.wait_ge(pe_step, 2)
            ch.step(nc.vector.tensor_scalar(grp[:, 4, :], ps[:, B:2 * B], 1e-5, None, ALU.add))
            assert ch.done.n == V_VAR, ch.done.n
            dve.wait_ge(act_step, 1)
            ch.step(nc.vector.reciprocal(grp[:, 6, :], grp[:, 5, :]))
            ch.step(nc.vector.tensor_scalar(grp[:, 6, :], grp[:, 6, :], vec[:, 0:1], None, ALU.mult))
            ch.step(nc.vector.tensor_tensor(grp[:, 7, :], grp[:, 0, :], grp[:, 6, :], ALU.mult))
            ch.step(nc.vector.tensor_scalar(grp[:, 7, :], grp[:, 7, :], -1.0, vec[:, 1:2], ALU.mult, ALU.add))
            for b in range(B):
                xb = X[:, b * HW:(b + 1) * HW]
                nc.vector.tensor_scalar(xb, xb, grp[:, 6, b:b + 1], grp[:, 7, b:b + 1], ALU.mult, ALU.add).then_inc(dve_step, 1)
                ch.done.n += 1
            ch.step(nc.vector.tensor_scalar(absw[:], t.qk_full[:], -1.0, None, ALU.mult))
            ch.step(nc.vector.tensor_tensor(absw[:], absw[:], t.qk_full[:], ALU.max))
            ch.step(nc.vector.tensor_scalar(vec[:, 6:8], vec[:, 0:2], -1.0, None, ALU.mult))
            ch.step(nc.vector.tensor_tensor(vec[:, 6:8], vec[:, 6:8], vec[:, 0:2], ALU.max))
            ch.step(nc.vector.scalar_tensor_tensor(vec[:, 6:7], vec[:, 6:7], float(HW * C // GROUPS) ** 0.5, vec[:, 7:8], ALU.mult, ALU.add))
            assert ch.done.n == V_ABS, ch.done.n
            ch.step(nc.vector.tensor_scalar(bnd[:, 0:2], vec[:, 4:6], -1.0, None, ALU.mult))
            ch.step(nc.vector.tensor_tensor(bnd[:, 0:2], bnd[:, 0:2], vec[:, 4:6], ALU.max))
            dve.wait_ge(pe_step, 3)
            ch.step(nc.vector.tensor_tensor(bnd[:, 2:4], ps[:, 8:10], bnd[:, 0:2], ALU.add))
            assert ch.done.n == V_BND, ch.done.n
            dve.wait_ge(pe_step, 4)
            ch.step(nc.vector.tensor_copy(row[:], ps[0:1, 16:272]))
            ch.step(nc.vector.tensor_reduce(top[:, 0:1], row[:], AX.X, ALU.max))
            ch.step(nc.vector.tensor_scalar(top[:, 1:2], top[:, 0:1], 1e-3, 1.0 / QBOUND, ALU.max, ALU.mult))
            assert ch.done.n == V_TOP, ch.done.n
            dve.wait_ge(pe_step, 5)
            ch.step(nc.vector.tensor_copy(t.qk_scale[:, 2:3], ps[:, 300:301]))
            ch.step(nc.vector.reciprocal(t.qk_scale[:, 0:1], t.qk_scale[:, 2:3]))
            ch.step(nc.vector.tensor_scalar(t.qk_scale[:, 1:2], t.qk_scale[:, 2:3], t.qk_scale[:, 2:3], float(C) ** -0.5, ALU.mult, ALU.mult))
            ch.step(nc.vector.tensor_scalar(t.qk_b[:], t.qk_b[:], t.qk_scale[0:96, 0:1], None, ALU.mult))
            dve.wait_ge(pe_step, 6)
            ch.step(nc.vector.tensor_tensor(t.out_b[:, 0:1], ps[:, 304:305], vec[:, 3:4], ALU.add))
            ch.step(nc.vector.tensor_copy(t.ident16[:], t.ident[:]))

        @block.tensor
        def _(pe):
            pe.wait_ge(const_in, 16 * len(loads))
            pe.wait_ge(dve_step, V_STAT)
            nc.tensor.matmul(ps[:, 0:B], group_avg[:], cst[:, :, 0], start=True, stop=True).then_inc(pe_step, 1)
            pe.wait_ge(dve_step, V_DEV)
            nc.tensor.matmul(ps[:, B:2 * B], group_avg[:], grp[:, 3, :], start=True, stop=True).then_inc(pe_step, 1)
            pe.wait_ge(dve_step, V_ABS)
            nc.tensor.matmul(ps[:, 8:9], absw[:, 0:128], vec[:, 6:7], start=True, stop=True)
            nc.tensor.matmul(ps[:, 9:10], absw[:, 128:256], vec[:, 6:7], start=True, stop=True).then_inc(pe_step, 1)
            pe.wait_ge(dve_step, V_BND)
            nc.tensor.matmul(ps[0:1, 16:144], bnd[:, 2:3], t.ident[:], start=True, stop=True)
            nc.tensor.matmul(ps[0:1, 144:272], bnd[:, 3:4], t.ident[:], start=True, stop=True).then_inc(pe_step, 1)
            pe.wait_ge(dve_step, V_TOP)
            nc.tensor.matmul(ps[:, 300:301], ones_row[:], top[:, 1:2], start=True, stop=True).then_inc(pe_step, 1)
            pe.wait_ge(dve_step, V_TOP + 1)
            nc.tensor.matmul(ps[:, 304:305], t.proj_w[:], vec[:, 2:3], start=True, stop=True).then_inc(pe_step, 1)


V_STAT = B * (CPB + 1)
V_DEV = V_STAT + 4
V_VAR = V_DEV + 1
V_ABS = V_VAR + 4 + B + 5
V_BND = V_ABS + 3
V_TOP = V_BND + 3


def attention(nc, X, t):
    with ExitStack() as ctx:
        sem = lambda n: ctx.enter_context(nc.semaphore(n))
        sb = lambda n, s, dt=F32: ctx.enter_context(nc.sbuf_tensor(n, s, dt))
        pst = lambda n, s: ctx.enter_context(nc.psum_tensor(n, s, F32))
        XB = sb("xn_batch", [128, HW])
        QS, KS = sb("q_stack", [128, HW], F16), sb("k_stack", [128, HW], F16)
        VS = sb("v_ones", [128, HEADS, ET, HD + 1])
        QK32 = sb("qk32", [96, 2, CH])
        P = sb("probs", [128, 4, 2, CH])
        AO = sb("att_out", [128, CH + HW])
        OS = sb("out_sums", [128, CH])
        R = sb("recip", [128, CH // 2])
        M8 = sb("block_max", [128, DT, CPB])
        M4 = sb("row_max", [128, DT])
        MC = sb("max_cols", [128, DT, 2], F16)
        S, A, O, M = pst("scores", [128, 4, CH]), pst("max_scores", [128, 2, CH]), pst("out_acc", [128, CH]), pst("misc", [128, CH])

        xb_ready, ready = sem("xb_ready"), sem("l0_ready")
        ev_mm, ev_done, split_done = sem("ev_mm"), sem("ev_done"), sem("split_done")
        a_mm, a_max = sem("a_mm"), sem("a_max")
        m_step, m_cols, m_rows, m_ready = sem("m_step"), sem("m_cols"), sem("m_rows"), sem("m_ready")
        b_mm, exp_done, pv_done, o_copied = sem("b_mm"), sem("exp_done"), sem("pv_done"), sem("o_copied")
        fin_mm, fin_rec, fin_done = sem("fin_mm"), sem("fin_rec"), sem("fin_done")
        pj_mm, pj_done = sem("pj_mm"), sem("pj_done")
        block = ctx.enter_context(nc.Block())
        EV = ET // 4 + HEADS * 2 * CPB
        AS = [(j * ABLK) // (PAIRS - 3) for j in range(PAIRS - 2)]
        a_of = lambda j: range(AS[j], AS[j + 1]) if j < PAIRS - 3 else range(0)

        @block.gpsimd
        def _(pool):
            nc.gpsimd.memset(VS[:, :, :, HD:HD + 1], 1.0).then_inc(ready, 1)
            pool.wait_ge(ready, 1)
            nc.gpsimd.memset(KS[96:128, :], MROW).then_inc(ready, 1)
            pool.wait_ge(ready, 2)
            nc.gpsimd.memset(OS[:], 1.0).then_inc(ready, 1)

        @block.vector
        def _(dve):
            for s, k in ((ev_done, 4), (a_max, 2), (exp_done, 2), (pv_done, 4), (o_copied, 1), (pj_done, 4), (split_done, 4)):
                nc.vector.memset(R[:, 0:1], 0.0).then_inc(s, k)
                dve.wait_ge(s, k)
            ev, split, amm, amax = Tally(4), Tally(4), Tally(), Tally(2)
            ms, mr, fmm, frec, pjm = Tally(), Tally(), Tally(), Tally(), Tally()

            def block_max(n):
                dve.wait_ge(a_mm, amm.next())
                nc.vector.reduce_max(M8[:, n // CPB, n % CPB:n % CPB + 1], A[:, n % 2, :], AX.X).then_inc(a_max, 1)
                amax.n += 1

            def row_max(c):
                dve.wait_ge(a_max, amax.value())
                nc.vector.reduce_max(M4[:], M8[:], AX.X).then_inc(m_step, 1)
                dve.wait_ge(m_step, ms.next())
                nc.vector.tensor_scalar(MC[:, :, 0], M4[:], -1.0 / MROW, None, ALU.mult).then_inc(m_step, 1)
                dve.wait_ge(m_step, ms.next())
                nc.vector.scalar_tensor_tensor(MC[:, :, 1], M4[:], -1.0 / MROW, MC[:, :, 0], ALU.mult, ALU.subtract).then_inc(m_cols, 1)
                dve.wait_ge(m_rows, mr.next())
                nc.vector.tensor_copy(QS[96:98, bass.ds(c * CH, CH)], M[96:98, :]).then_inc(m_ready, 1)

            def finish(h, c, half):
                q = slice(HD * h, HD * h + HD)
                dve.wait_ge(fin_mm, fmm.next())
                nc.vector.reciprocal(R[q, :], M[q, 256:512]).then_inc(fin_rec, 1)
                dve.wait_ge(fin_rec, frec.next())
                nc.vector.tensor_tensor(AO[q, bass.ds(c * CH + half * 256, 256)], M[q, 0:256], R[q, :], ALU.mult).then_inc(fin_done, 1)

            def chunk(h, c, more):
                for j in range(PAIRS):
                    for n in (a_of(j) if more else ()):
                        block_max(n)
                    if j in (2, 3):
                        finish(h, c, j - 2)
                if more:
                    row_max(c + 1)

            per = [(ev, EV - ET // 4), (split, 4 * CPB * HEADS), (amm, ABLK * CPB * HEADS), (amax, ABLK * CPB * HEADS),
                   (ms, 2 * CPB * HEADS), (mr, CPB * HEADS), (fmm, 2 * (CPB + 1) * HEADS), (frec, 2 * (CPB + 1) * HEADS), (pjm, CPB)]
            ev.n += 0
            evb = Tally(4)
            per[0] = (evb, EV)
            with counted_loop(dve, B, *per) as b:
                dve.wait_ge(pj_done, pjm.value(4))
                nc.vector.tensor_copy(XB[:], X[:, bass.ds(b * HW, HW)]).then_inc(xb_ready, 1)
                evb.n += ET // 4
                for h in range(HEADS):
                    for n in range(2 * CPB):
                        k, which = n // 2, n % 2
                        st = (QS, KS)[which]
                        cols = slice(k * CH, (k + 1) * CH)
                        lo = slice(32, 64) if which == 0 else slice(64, 96)
                        dve.wait_ge(ev_done, evb.next())
                        nc.vector.tensor_copy(st[0:96, cols], QK32[:, n % 2, :]).then_inc(split_done, 1)
                        dve.wait_ge(split_done, split.next())
                        nc.vector.tensor_tensor(st[lo, cols], QK32[lo, n % 2, :], st[lo, cols], ALU.subtract).then_inc(split_done, 1)
                        split.n += 1
                    for n in range(ABLK):
                        block_max(n)
                    row_max(0)
                    with counted_loop(dve, CPB - 1, (amm, ABLK), (amax, ABLK), (ms, 2), (mr, 1), (fmm, 2), (frec, 2)) as c:
                        chunk(h, c, True)
                    chunk(h, CPB - 1, False)
                    finish(h, CPB, 0)
                    finish(h, CPB, 1)
                for k in range(CPB):
                    dve.wait_ge(pj_mm, pjm.next())
                    nc.vector.scalar_tensor_tensor(X[:, bass.ds(b * HW + k * CH, CH)], S[:, k % 4, :], t.out_b[:, 0:1],
                                                   XB[:, k * CH:(k + 1) * CH], ALU.add, ALU.add).then_inc(pj_done, 1)

        @block.scalar
        def _(act):
            act.wait_ge(ready, 3)
            evm, sp_, bm, ex, pv = Tally(), Tally(4), Tally(), Tally(2), Tally(4)
            ev_own = Tally(4)
            pv_free, spf = Tally(0), Tally(0)

            def exps(h):
                for j in range(PAIRS):
                    act.wait_ge(b_mm, bm.next())
                    act.wait_ge(pv_done, pv_free.next())
                    nc.scalar.activation(P[:, j % 4, :, :], S[:, 2 * (j % 2):2 * (j % 2) + 2, :], ACT.Exp,
                                         scale=t.qk_scale[:, 1:2]).then_inc(exp_done, 1)
                act.wait_ge(pv_done, pv_free.value(4))
                nc.scalar.copy(OS[0:HD + 1, :], O[0:HD + 1, :])
                nc.scalar.copy(OS[64:64 + HD + 1, :], O[64:64 + HD + 1, :]).then_inc(o_copied, 1)

            with counted_loop(act, B, (evm, EV), (spf, 2 * CPB * HEADS * 2), (bm, PAIRS * CPB * HEADS), (pv_free, PAIRS * CPB * HEADS)) as b:
                for g in range(ET // 4):
                    act.wait_ge(ev_mm, evm.next())
                    nc.scalar.copy(VS[:, :, 4 * g:4 * g + 4, 0:HD].rearrange("p h t c -> p t h c"),
                                   S[:, g % 4, :].rearrange("p (t h c) -> p t h c", t=4, h=HEADS)).then_inc(ev_done, 1)
                for h in range(HEADS):
                    for n in range(2 * CPB):
                        act.wait_ge(ev_mm, evm.next())
                        spf.n += 2
                        act.wait_ge(split_done, spf.value())
                        nc.scalar.activation(QK32[:, n % 2, :], S[0:96, n % 4, :], ACT.Identity,
                                             bias=t.qk_b[:, 2 * h + n % 2:2 * h + n % 2 + 1],
                                             scale=t.qk_scale[0:96, 0:1]).then_inc(ev_done, 1)
                    with counted_loop(act, CPB, (bm, PAIRS), (pv_free, PAIRS)) as c:
                        exps(h)

        @block.tensor
        def _(pe):
            pe.wait_ge(ready, 3)
            xb, evf, spl, af = Tally(), Tally(0), Tally(4), Tally(0)
            mc, mrd, exf, exd, ocf, ocd, fdn, pjf = Tally(), Tally(), Tally(0), Tally(2), Tally(0), Tally(1), Tally(), Tally(0)

            def max_block(c, n):
                pe.wait_ge(a_max, af.next())
                nc.tensor.matmul(A[:, n % 2, :], QS[0:96, bass.ds(c * CH + (n // CPB) * 128, 128)],
                                 KS[0:96, (n % CPB) * CH:(n % CPB + 1) * CH], start=True, stop=True).then_inc(a_mm, 1)

            def max_rows():
                pe.wait_ge(m_cols, mc.next())
                for k in range(DT):
                    m = nc.tensor.matmul(M[96:98, k * 128:(k + 1) * 128], MC[:, k, :], t.ident16[:], start=True, stop=True)
                m.then_inc(m_rows, 1)

            def pair_scores(c, j):
                pe.wait_ge(exp_done, exf.next())
                for i in range(2):
                    e = 2 * j + i
                    m = nc.tensor.matmul(S[:, 2 * (j % 2) + i, :], KS[0:98, e * 128:(e + 1) * 128],
                                         QS[0:98, bass.ds(c * CH, CH)], start=True, stop=True)
                m.then_inc(b_mm, 1)

            def pair_out(h, j):
                pe.wait_ge(exp_done, exd.next())
                if j == 0:
                    pe.wait_ge(o_copied, ocf.next())
                for i in range(2):
                    m = nc.tensor.matmul(O[64 * i:64 * i + HD + 1, :], VS[:, h, 2 * j + i, :], P[:, j % 4, i, :],
                                         start=(j == 0), stop=(j == PAIRS - 1))
                m.then_inc(pv_done, 1)

            def finish(h, half):
                if half == 0:
                    pe.wait_ge(o_copied, ocd.value())
                if half == 1:
                    pe.wait_ge(fin_done, fdn.value())
                q = slice(HD * h, HD * h + HD)
                nc.tensor.matmul(M[q, 0:256], t.sel[0:97, 0, :], OS[0:97, half * 256:half * 256 + 256], start=True, stop=True)
                nc.tensor.matmul(M[q, 256:512], t.sel[0:97, 1, :], OS[0:97, half * 256:half * 256 + 256], start=True, stop=True).then_inc(fin_mm, 1)
                fdn.n += 1

            def chunk(h, c, more):
                pe.wait_ge(m_ready, mrd.next())
                for j in range(PAIRS):
                    pair_scores(c, j)
                    for n in (a_of(j) if more else ()):
                        max_block(c + 1, n)
                    if j >= 1:
                        pair_out(h, j - 1)
                    if j in (2, 3):
                        finish(h, j - 2)
                pair_out(h, PAIRS - 1)
                ocd.n += 1
                if more:
                    pe.wait_ge(fin_done, fdn.value())
                    max_rows()

            with counted_loop(pe, B, (xb, 1), (evf, EV), (spl, 4 * CPB * HEADS), (af, ABLK * CPB * HEADS), (mc, CPB * HEADS), (mrd, CPB * HEADS),
                              (exf, PAIRS * CPB * HEADS), (exd, PAIRS * CPB * HEADS), (ocf, CPB * HEADS), (ocd, CPB * HEADS),
                              (fdn, 2 * (CPB + 1) * HEADS), (pjf, CPB)) as b:
                pe.wait_ge(xb_ready, xb.next())
                pe.wait_ge(pj_done, pjf.value(4))
                for g in range(ET // 4):
                    pe.wait_ge(ev_done, evf.next())
                    for k in range(4):
                        e = 4 * g + k
                        m = nc.tensor.matmul(S[:, g % 4, k * 128:(k + 1) * 128], XB[:, e * 128:(e + 1) * 128], t.v_w[:], start=True, stop=True)
                    m.then_inc(ev_mm, 1)
                for h in range(HEADS):
                    for n in range(2 * CPB):
                        pe.wait_ge(ev_done, evf.next())
                        nc.tensor.matmul(S[0:96, n % 4, :], t.qk_w[:, h, n % 2, :], XB[:, (n // 2) * CH:(n // 2 + 1) * CH],
                                         start=True, stop=True).then_inc(ev_mm, 1)
                    spl.n += 4 * CPB
                    pe.wait_ge(split_done, spl.value())
                    for n in range(ABLK):
                        max_block(0, n)
                    if h > 0:
                        pe.wait_ge(fin_done, fdn.value())
                    max_rows()
                    with counted_loop(pe, CPB - 1, (af, ABLK), (mc, 1), (mrd, 1), (exf, PAIRS), (exd, PAIRS), (ocf, 1), (ocd, 1), (fdn, 2)) as c:
                        chunk(h, c, True)
                    chunk(h, CPB - 1, False)
                    pe.wait_ge(fin_done, fdn.value())
                    finish(h, 0)
                    finish(h, 1)
                pe.wait_ge(fin_done, fdn.value())
                for k in range(CPB):
                    pe.wait_ge(pj_done, pjf.next())
                    nc.tensor.matmul(S[:, k % 4, :], t.proj_w[:], AO[:, CH + k * CH:CH + (k + 1) * CH], start=True, stop=True).then_inc(pj_mm, 1)


PAD = H + 2
ROWS = CH // W
TAPS = 9


def binary_conv(nc, d, X):
    with ExitStack() as ctx:
        sem = lambda n: ctx.enter_context(nc.semaphore(n))
        sb = lambda n, s, dt=F32: ctx.enter_context(nc.sbuf_tensor(n, s, dt))
        XS = sb("x_sign", [128, B, PAD, PAD], BF16)
        Y = sb("conv_sums", [128, N], F16)
        NEG = sb("neg_part", [128, 2, HW])
        wt, wr = sb("conv_wt", [128, TAPS * 128]), sb("conv_wr", [128, TAPS * 128])
        ws = sb("conv_wsign", [128, TAPS, 128], BF16)
        vec = sb("l1_vec", [128, 6])
        v = sb("l1_tmp", [128, 12])
        stats = sb("bn_stats", [128, B * CPB, 6])
        S = ctx.enter_context(nc.psum_tensor("conv_ps", [128, CPB, CH], F32))
        l1_in, edges, signed, wsigned = sem("l1_in"), sem("edges"), sem("signed"), sem("wsigned")
        cv_mm, cv_out, cv_stat, dve_step, act_step, relu_done, l1_done = (sem(n) for n in
            ("cv_mm", "cv_out", "cv_stat", "l1_dve", "l1_act", "relu_done", "l1_done"))
        block = ctx.enter_context(nc.Block())

        @block.sync
        def _(sp):
            sp.dma_start(vec[:], d["l1_vec"]).then_inc(l1_in, 16)
            sp.dma_start(wt[:], d["l1_wt"]).then_inc(l1_in, 16)
            sp.dma_start(wr[:], d["l1_wr"]).then_inc(l1_in, 16)

        @block.gpsimd
        def _(pool):
            for k, edge in enumerate((XS[:, :, 0, :], XS[:, :, PAD - 1, :], XS[:, :, 1:PAD - 1, 0:1], XS[:, :, 1:PAD - 1, PAD - 1:PAD])):
                nc.gpsimd.memset(edge, 0.0).then_inc(edges, 1)
                pool.wait_ge(edges, k + 1)

        @block.tensor
        def _(pe):
            pe.wait_ge(edges, 4)
            pe.wait_ge(wsigned, 1)
            for b in range(B):
                pe.wait_ge(signed, b + 1)
                for k in range(CPB):
                    if b > 0:
                        pe.wait_ge(cv_out, (b - 1) * CPB + k + 1)
                    for tap in range(TAPS):
                        dy, dx = tap // 3, tap % 3
                        m = nc.tensor.matmul(S[:, k, :], ws[:, tap, :], XS[:, b, k * ROWS + dy:k * ROWS + dy + ROWS, dx:dx + W],
                                             start=(tap == 0), stop=(tap == TAPS - 1))
                    m.then_inc(cv_mm, 1)

        @block.scalar
        def _(act):
            act.wait_ge(l1_in, 48)
            nc.scalar.activation(ws[:].rearrange("p a b -> p (a b)"), wt[:], ACT.Sign).then_inc(wsigned, 1)
            for b in range(B):
                nc.scalar.activation(XS[:, b, 1:H + 1, 1:W + 1], X[:, b * HW:(b + 1) * HW].rearrange("p (h w) -> p h w", h=H),
                                     ACT.Sign, bias=vec[:, 0:1]).then_inc(signed, 1)
            for k in range(B * CPB):
                act.wait_ge(cv_mm, k + 1)
                nc.scalar.copy(Y[:, k * CH:(k + 1) * CH], S[:, k % CPB, :]).then_inc(cv_out, 1)
            act.wait_ge(dve_step, V_VARY)
            nc.scalar.activation(v[:, 4:5], v[:, 3:4], ACT.Sqrt).then_inc(act_step, 1)
            for b in range(B):
                act.wait_ge(relu_done, 2 * b + 2)
                xb = X[:, b * HW:(b + 1) * HW]
                nc.scalar.activation(xb, xb, ACT.Identity, bias=v[:, 9:10]).then_inc(act_step, 1)

        @block.vector
        def _(dve):
            ch = Chain(dve, dve_step)
            dve.wait_ge(l1_in, 48)
            ch.step(nc.vector.tensor_reduce(v[:, 0:1], wr[:], AX.X, ALU.add, apply_absolute_value=True))
            ch.step(nc.vector.tensor_scalar(v[:, 0:1], v[:, 0:1], 1.0 / (TAPS * C), None, ALU.mult))
            for k in range(B * CPB):
                dve.wait_ge(cv_out, k + 1)
                nc.vector.bn_stats(stats[:, k, :], Y[:, k * CH:(k + 1) * CH]).then_inc(cv_stat, 1)
            dve.wait_ge(cv_stat, B * CPB)
            ch.step(nc.vector.bn_aggr(v[:, 1:3], stats[:].rearrange("p k s -> p (k s)")))
            ch.step(nc.vector.tensor_scalar(v[:, 3:4], v[:, 2:3], v[:, 0:1], v[:, 0:1], ALU.mult, ALU.mult))
            ch.step(nc.vector.tensor_scalar(v[:, 3:4], v[:, 3:4], 1e-5, None, ALU.add))
            assert ch.done.n == V_VARY
            dve.wait_ge(act_step, 1)
            ch.step(nc.vector.reciprocal(v[:, 5:6], v[:, 4:5]))
            ch.step(nc.vector.tensor_scalar(v[:, 6:7], v[:, 5:6], v[:, 0:1], vec[:, 1:2], ALU.mult, ALU.mult))
            ch.step(nc.vector.tensor_scalar(v[:, 7:8], v[:, 6:7], v[:, 1:2], -1.0, ALU.mult, ALU.mult))
            ch.step(nc.vector.tensor_scalar(v[:, 8:9], v[:, 7:8], vec[:, 2:3], vec[:, 3:4], ALU.add, ALU.add))
            ch.step(nc.vector.tensor_scalar(v[:, 9:10], v[:, 8:9], vec[:, 5:6], None, ALU.add))
            ch.step(nc.vector.tensor_scalar(v[:, 10:11], vec[:, 4:5], -1.0, None, ALU.add))
            for b in range(B + 1):
                if b < B:
                    xb = X[:, b * HW:(b + 1) * HW]
                    nc.vector.scalar_tensor_tensor(xb, Y[:, b * HW:(b + 1) * HW], v[:, 6:7], xb, ALU.mult, ALU.add).then_inc(relu_done, 1)
                    dve.wait_ge(relu_done, 2 * b + 1)
                    if b >= 2:
                        dve.wait_ge(l1_done, b - 1)
                    nc.vector.tensor_scalar(NEG[:, b % 2, :], xb, v[:, 8:9], 0.0, ALU.add, ALU.min).then_inc(relu_done, 1)
                if b >= 1:
                    xb = X[:, (b - 1) * HW:b * HW]
                    dve.wait_ge(relu_done, 2 * b)
                    dve.wait_ge(act_step, 1 + b)
                    nc.vector.scalar_tensor_tensor(xb, NEG[:, (b - 1) % 2, :], v[:, 10:11], xb, ALU.mult, ALU.add).then_inc(l1_done, 1)


V_VARY = 5


WS = 8
NW = W // WS
WT = WS * WS
DI = 256
DH = DI // 128
NS = 16
SG = 2
GR = NS // SG
DTR = 8
KC = 4
NCH = B * CPB


def mamba(nc, d, X):
    with ExitStack() as ctx:
        sem = lambda n: ctx.enter_context(nc.semaphore("l2_" + n))
        sb = lambda n, s, dt=F32: ctx.enter_context(nc.sbuf_tensor("l2_" + n, s, dt))
        w_in, w_dt, w_out = sb("w_in", [128, 2 * DI]), sb("w_dt", [128, DH, DI]), sb("w_out", [128, DH, C])
        w_bc, onehot = sb("w_bc", [128, DH, 3 * 2 * NS]), sb("onehot", [96, 2 * NS, 128], BF16)
        taps = sb("taps", [128, DH * KC, 128])
        ident, avg, ones = sb("ident", [128, 128]), sb("avg", [128, 128]), sb("ones", [128, 128])
        Am = sb("A", [128, DH * NS])
        vec = sb("vec", [128, 22])
        with ExitStack() as c1:
            sb1 = lambda n, s, dt=F32: c1.enter_context(nc.sbuf_tensor("l2_" + n, s, dt))
            wdr, dtw, oh32 = sb1("wdr", [DTR, DI]), sb1("dtw", [DTR, DI]), sb1("oh32", [96, 2 * NS])
            ps = c1.enter_context(nc.psum_tensor("l2_setup_ps", [128, 2, 512], F32))
            w_loaded, s_pe, s_act, s_dve = sem("w_loaded"), sem("s_pe"), sem("s_act"), sem("s_dve")
            block = c1.enter_context(nc.Block())
            loads = [(w_in, "l2_w_in"), (w_out, "l2_w_out"), (w_bc, "l2_w_bc"), (ident, "ident"), (Am, "l2_alog"), (vec, "l2_vec"),
                     (wdr, "l2_wdr"), (dtw, "l2_dtw"), (oh32, "l2_onehot")]

            @block.sync
            def _(sp):
                for dst, name in loads:
                    sp.dma_start(dst[:], d[name]).then_inc(w_loaded, 16)

            @block.tensor
            def _(pe):
                pe.wait_ge(w_loaded, 16 * len(loads))
                for h in range(DH):
                    nc.tensor.matmul(ps[:, h, 0:DI], wdr[:, h * 128:(h + 1) * 128], dtw[:], start=True, stop=True)
                for k in range(4):
                    m = nc.tensor.matmul(ps[:, 0, 300 + k:301 + k], w_in[:, k * 128:(k + 1) * 128], vec[:, 13:14], start=True, stop=True)
                m.then_inc(s_pe, 1)

            @block.scalar
            def _(act):
                act.wait_ge(w_loaded, 16 * len(loads))
                nc.scalar.activation(Am[:], Am[:], ACT.Exp).then_inc(s_act, 1)

            @block.vector
            def _(dve):
                ch = Chain(dve, s_dve)
                dve.wait_ge(w_loaded, 16 * len(loads))
                ch.step(nc.vector.memset(avg[:], 1.0 / C))
                ch.step(nc.vector.memset(ones[:], 1.0))
                ch.step(nc.vector.tensor_copy(onehot[:], oh32[:].unsqueeze(2).to_broadcast([96, 2 * NS, 128])))
                for k in range(DH * KC):
                    ch.step(nc.vector.tensor_scalar(taps[:, k, :], ident[:], vec[:, 14 + k:15 + k], None, ALU.mult))
                dve.wait_ge(s_pe, 1)
                ch.step(nc.vector.tensor_copy(w_dt[:], ps[:, :, 0:DI]))
                ch.step(nc.vector.tensor_tensor(vec[:, 8:12], vec[:, 8:12], ps[:, 0, 300:304], ALU.add))
                ch.step(nc.vector.tensor_scalar(w_in[:], w_in[:], vec[:, 12:13], None, ALU.mult))
                dve.wait_ge(s_act, 1)
                ch.step(nc.vector.tensor_scalar(Am[:], Am[:], -1.0, None, ALU.mult))

        XCEN, XSQ, TN, DIAG = sb("x_cen", [128, CH]), sb("x_sq", [128, CH]), sb("x_norm", [128, CH]), sb("rstd_diag", [128, 4, 128])
        std = sb("std", [128, 4])
        XP = sb("xi_padded", [128, DH, NW, KC - 1 + WT])
        XC, ZS = sb("xc", [128, 2, DH, CH]), sb("z_silu", [128, 2, DH, CH])
        DEL, DTX = sb("delta", [128, 2, DH, CH]), sb("delta_x", [128, 2, DH, CH])
        EX, UU = sb("exp_abs", [128, DH, CH]), sb("one_plus", [128, DH, CH])
        BCS, R1, MID = sb("bc_split", [96, 2, CH], BF16), sb("bc_rest", [96, CH]), sb("bc_mid", [96, CH], BF16)
        DA, HB, HC = sb("decay", [128, 2, DH, SG, CH]), sb("state", [128, 2, DH, SG, CH]), sb("state_c", [128, 2, DH, SG, CH])
        CB = sb("c_rows", [128, 2, SG, CH])
        YG, OT = sb("y_gated", [128, DH, CH]), sb("out_rows", [128, CH])
        pst = lambda n, s: ctx.enter_context(nc.psum_tensor("l2_" + n, s, F32))
        PB, PC, PY, PF = pst("b_rows", [128, SG, CH]), pst("c_rows_ps", [128, SG, CH]), pst("y_acc", [128, DH, CH]), pst("front", [128, 2, CH])

        zeroed = sem("zeroed")
        mu_mm, centred, squared, var_mm, std_done, diag, rs_mm, normed = (sem(n) for n in
            ("mu_mm", "centred", "squared", "var_mm", "std_done", "diag", "rs_mm", "normed"))
        in_mm, xp_done, cv_mm, xc_done, z_mm, zs_done, bc_mm, split, dp_mm = (sem(n) for n in
            ("in_mm", "xp_done", "cv_mm", "xc_done", "z_mm", "zs_done", "bc_mm", "split", "dp_mm"))
        abs_done, relu_done, exp_done, plus_done, ln_done, delta, dtx_done = (sem(n) for n in
            ("abs_done", "relu_done", "exp_done", "plus_done", "ln_done", "delta", "dtx_done"))
        bb_mm, cb_mm, cb_done, da_done, b_done, scanned, hc_done, acc_mm = (sem(n) for n in
            ("bb_mm", "cb_mm", "cb_done", "da_done", "b_done", "scanned", "hc_done", "acc_mm"))
        gated, op_mm, ot_done, added = sem("gated"), sem("op_mm"), sem("ot_done"), sem("added")
        block = ctx.enter_context(nc.Block())

        def chunks(eng, step, per_chunk):
            step(0, 0, False, True)
            with counted_loop(eng, (NCH - 2) // 2, *[(t, 2 * k) for t, k in per_chunk]) as turn:
                step(turn * 2 + 1, 1, True, True)
                step(turn * 2 + 2, 0, True, True)
            step(NCH - 1, 1, True, False)

        cols = lambda n: bass.ds(n * CH, CH)
        windows = lambda ap: ap.rearrange("p (h n w) -> p h n w", h=WS, n=NW)
        by_window = lambda ap: ap.rearrange("p (n h w) -> p h n w", n=NW, h=WS)

        @block.tensor
        def _(pe):
            relu, sq, dg, nrm, xp, xc, zs, spl = Tally(1), Tally(), Tally(), Tally(), Tally(), Tally(), Tally(), Tally()
            bfree, cfree, hcd, gt, ad = Tally(0), Tally(0), Tally(2), Tally(), Tally()
            pe.wait_ge(zeroed, 6)

            def front(n, q, g):
                if g == 0:
                    pe.wait_ge(relu_done, relu.value())
                    relu.n += DH
                    nc.tensor.matmul(PF[:, 1, :], avg[:], X[:, cols(n)], start=True, stop=True).then_inc(mu_mm, 1)
                if g == 1:
                    pe.wait_ge(squared, sq.next())
                    for k in range(4):
                        m = nc.tensor.matmul(PF[:, 1, k:k + 1], XSQ[:, k * 128:(k + 1) * 128], avg[:, 0:1], start=True, stop=True)
                    m.then_inc(var_mm, 1)
                if g == 2:
                    dg.n += 1
                    pe.wait_ge(diag, dg.next())
                    nc.tensor.matmul(PF[:, 1, :], ones[:], DIAG[:].rearrange("p k c -> p (k c)"), start=True, stop=True).then_inc(rs_mm, 1)
                if g == 3:
                    pe.wait_ge(normed, nrm.next())
                    for h in range(DH):
                        nc.tensor.matmul(PF[:, h, :], w_in[:, h * 128:(h + 1) * 128], TN[:], start=True, stop=True).then_inc(in_mm, 1)
                if g == 4:
                    for h in range(DH):
                        pe.wait_ge(xp_done, xp.next())
                        for k in range(KC):
                            m = nc.tensor.matmul(PF[:, h, :], taps[:, h * KC + k, :], XP[:, h, :, k:k + WT], start=(k == 0), stop=(k == KC - 1))
                        m.then_inc(cv_mm, 1)
                    for h in range(DH):
                        pe.wait_ge(xc_done, xc.next())
                        nc.tensor.matmul(PF[:, h, :], w_in[:, DI + h * 128:DI + (h + 1) * 128], TN[:], start=True, stop=True).then_inc(z_mm, 1)
                if g == 5:
                    pe.wait_ge(zs_done, zs.next())
                    for h in range(DH):
                        m = nc.tensor.matmul(PF[0:96, 0, :], w_bc[:, h, :], XC[:, q, h, :], start=(h == 0), stop=(h == DH - 1))
                    m.then_inc(bc_mm, 1)
                    pe.wait_ge(zs_done, zs.next())
                if g == 5 or g == 6:
                    o = g - 5
                    if o == 1:
                        spl.n += 5
                        pe.wait_ge(split, spl.value())
                    for h in range(DH):
                        m = nc.tensor.matmul(PF[:, 1 - o, :], w_dt[:, h, o * 128:(o + 1) * 128], XC[:, q, h, :], start=(h == 0), stop=(h == DH - 1))
                    m.then_inc(dp_mm, 1)

            def accumulate(k):
                pe.wait_ge(hc_done, hcd.next())
                if k == 0:
                    gt_wait()
                for h in range(DH):
                    for i in range(SG):
                        m = nc.tensor.matmul(PY[:, h, :], ident[:], HC[:, k % 2, h, i, :], start=(k == 0 and i == 0), stop=(k == GR - 1 and i == SG - 1))
                m.then_inc(acc_mm, 1)

            state = {"first": True}

            def gt_wait():
                if not state["first"]:
                    pe.wait_ge(gated, gt.value())

            def project_out():
                gt.n += 3
                pe.wait_ge(gated, gt.value())
                for h in range(DH):
                    m = nc.tensor.matmul(PF[:, 0, :], w_out[:, h, :], YG[:, h, :], start=(h == 0), stop=(h == DH - 1))
                m.then_inc(op_mm, 1)

            def chunk(i, q, back, more):
                for g in range(GR):
                    pe.wait_ge(b_done, bfree.next())
                    for k in range(SG):
                        m = nc.tensor.matmul(PB[:, k, :], onehot[:, g * SG + k, :], BCS[:, q, :], start=True, stop=True)
                    m.then_inc(bb_mm, 1)
                    pe.wait_ge(cb_done, cfree.next())
                    for k in range(SG):
                        m = nc.tensor.matmul(PC[:, k, :], onehot[:, NS + g * SG + k, :], BCS[:, q, :], start=True, stop=True)
                    m.then_inc(cb_mm, 1)
                    if g < 2:
                        if back:
                            accumulate(GR - 2 + g)
                    else:
                        if g == 2 and back:
                            project_out()
                        accumulate(g - 2)
                    if more:
                        if g == 3 and back:
                            pe.wait_ge(ot_done, ad.next())
                        front(i + 1, 1 - q, g)
                state["first"] = False
                if not more:
                    ad.n += 1

            for g in range(GR - 1):
                front(0, 0, g)
            pe.wait_ge(split, spl.value())
            chunks(pe, chunk, [(relu, DH), (sq, 1), (dg, 2), (nrm, 1), (xp, DH), (xc, DH), (zs, 2), (spl, 5),
                               (bfree, GR), (cfree, GR), (hcd, GR), (gt, 3), (ad, 1)])
            accumulate(GR - 2)
            accumulate(GR - 1)
            project_out()

        @block.scalar
        def _(act):
            cen, var, inm, cvm, zm, dpm, pls, dlt = (Tally() for _ in range(8))
            cbm, hcf, scf, opm, ab, ln = Tally(), Tally(0), Tally(0), Tally(), Tally(), Tally()
            act.wait_ge(zeroed, 6)

            def front(n, q, g):
                if g == 0:
                    act.wait_ge(centred, cen.next())
                    nc.scalar.activation(XSQ[:], XCEN[:], ACT.Square).then_inc(squared, 1)
                if g == 1:
                    act.wait_ge(var_mm, var.next())
                    nc.scalar.activation(std[:], PF[:, 1, 0:4], ACT.Sqrt, bias=vec[:, 0:1]).then_inc(std_done, 1)
                if g == 3:
                    for h in range(DH):
                        act.wait_ge(in_mm, inm.next())
                        nc.scalar.activation(XP[:, h, :, KC - 1:], PF[:, h, :].rearrange("p (n t) -> p n t", n=NW), ACT.Identity,
                                             bias=vec[:, 8 + h:9 + h]).then_inc(xp_done, 1)
                if g == 4:
                    for h in range(DH):
                        act.wait_ge(cv_mm, cvm.next())
                        nc.scalar.activation(XC[:, q, h, :], PF[:, h, :], ACT.Silu, bias=vec[:, 2 + h:3 + h]).then_inc(xc_done, 1)
                    for h in range(DH):
                        act.wait_ge(z_mm, zm.next())
                        nc.scalar.activation(ZS[:, q, h, :], PF[:, h, :], ACT.Silu, bias=vec[:, 10 + h:11 + h]).then_inc(zs_done, 1)
                if g == 5 or g == 6:
                    o = g - 5
                    act.wait_ge(dp_mm, dpm.next())
                    nc.scalar.activation(EX[:, o, :], PF[:, 1 - o, :], ACT.Abs, bias=vec[:, 4 + o:5 + o]).then_inc(abs_done, 1)
                if g == 6:
                    ab.n += DH
                    act.wait_ge(abs_done, ab.value())
                    nc.scalar.activation(EX[:], EX[:], ACT.Exp, scale=-1.0).then_inc(exp_done, 1)
                if g == 7:
                    act.wait_ge(plus_done, pls.next())
                    nc.scalar.activation(DEL[:, q], UU[:], ACT.Ln).then_inc(ln_done, 1)

            def chunk(i, q, back, more):
                dlt.n += 3
                act.wait_ge(delta, dlt.value())
                for g in range(GR):
                    act.wait_ge(scanned, scf.next())
                    for h in range(DH):
                        for k in range(SG):
                            e = nc.scalar.activation(DA[:, g % 2, h, k, :].rearrange("p (n t) -> p n t", n=NW)[:, :, 1:],
                                                     DEL[:, q, h, :].rearrange("p (n t) -> p n t", n=NW)[:, :, 1:], ACT.Exp,
                                                     scale=Am[:, h * NS + g * SG + k:h * NS + g * SG + k + 1])
                    e.then_inc(da_done, 1)
                    act.wait_ge(cb_mm, cbm.next())
                    act.wait_ge(hc_done, hcf.next())
                    nc.scalar.copy(CB[:, g % 2], PC[:]).then_inc(cb_done, 1)
                    if g == 2 and back:
                        act.wait_ge(op_mm, opm.next())
                        nc.scalar.activation(windows(OT[:]), by_window(PF[:, 0, :]), ACT.Identity, bias=vec[:, 1:2]).then_inc(ot_done, 1)
                    if more:
                        front(i + 1, 1 - q, g)

            for g in range(GR):
                front(0, 0, g)
            chunks(act, chunk, [(cen, 1), (var, 1), (inm, DH), (cvm, DH), (zm, DH), (dpm, DH), (pls, 1), (dlt, 3),
                                (cbm, GR), (hcf, GR), (scf, GR), (opm, 1), (ab, DH)])
            act.wait_ge(op_mm, opm.next())
            nc.scalar.activation(windows(OT[:]), by_window(PF[:, 0, :]), ACT.Identity, bias=vec[:, 1:2]).then_inc(ot_done, 1)

        @block.vector
        def _(dve):
            zero = [XP[:, :, :, 0:KC - 1]] + [DA[:, s, h].rearrange("p k (n t) -> p (k n) t", n=NW)[:, :, 0:1] for s in range(2) for h in range(DH)]
            for z in zero:
                nc.vector.memset(z, 0.0).then_inc(zeroed, 1)
            nc.vector.memset(vec[:, 0:1], 1e-5).then_inc(zeroed, 1)
            for n, (s, k) in enumerate(((relu_done, 1), (b_done, 1), (cb_done, 1), (scanned, 2), (hc_done, 2), (acc_mm, 2))):
                nc.vector.memset(std[:, 0:1], 0.0).then_inc(s, k)
                dve.wait_ge(s, k)
            mum, std_, dg, rsm, bcm, spl, abs_, rl, ex, ln, dl = (Tally() for _ in range(11))
            bbm, hcf, bd, da, scn, accd, gt, otd, rlt = Tally(), Tally(0), Tally(1), Tally(), Tally(2), Tally(2), Tally(), Tally(), Tally(1)
            addn = Tally()

            def front(n, q, g):
                if g == 0:
                    dve.wait_ge(mu_mm, mum.next())
                    nc.vector.tensor_tensor(XCEN[:], X[:, cols(n)], PF[:, 1, :], ALU.subtract).then_inc(centred, 1)
                if g == 1:
                    dve.wait_ge(std_done, std_.next())
                    nc.vector.reciprocal(std[:], std[:]).then_inc(diag, 1)
                    dve.wait_ge(diag, dg.next())
                    nc.vector.tensor_tensor(DIAG[:], ident[:].unsqueeze(1).to_broadcast([128, 4, 128]), std[:].unsqueeze(2).to_broadcast([128, 4, 128]),
                                            ALU.mult).then_inc(diag, 1)
                    dg.n += 1
                if g == 2:
                    dve.wait_ge(rs_mm, rsm.next())
                    nc.vector.tensor_tensor(by_window(TN[:]), windows(XCEN[:]), windows(PF[:, 1, :]), ALU.mult).then_inc(normed, 1)
                if g == 5:
                    dve.wait_ge(bc_mm, bcm.next())
                    nc.vector.tensor_copy(BCS[:, q, :], PF[0:96, 0, :]).then_inc(split, 1)
                    dve.wait_ge(split, spl.next())
                    nc.vector.tensor_tensor(R1[:], PF[0:96, 0, :], BCS[:, q, :], ALU.subtract).then_inc(split, 1)
                    dve.wait_ge(split, spl.next())
                    nc.vector.tensor_copy(BCS[32:64, q, :], R1[32:64, :]).then_inc(split, 1)
                    nc.vector.tensor_copy(MID[64:96, :], R1[64:96, :]).then_inc(split, 1)
                    spl.n += 2
                    dve.wait_ge(split, spl.value())
                    nc.vector.tensor_tensor(BCS[64:96, q, :], R1[64:96, :], MID[64:96, :], ALU.subtract).then_inc(split, 1)
                    spl.n += 1
                if g == 5 or g == 6:
                    o = g - 5
                    dve.wait_ge(abs_done, abs_.next())
                    nc.vector.tensor_scalar(DTX[:, q, o, :], PF[:, 1 - o, :], vec[:, 4 + o:5 + o], 0.0, ALU.add, ALU.max).then_inc(relu_done, 1)
                    rlt.n += 1
                if g == 6:
                    dve.wait_ge(exp_done, ex.next())
                    nc.vector.tensor_scalar(UU[:], EX[:], 1.0, None, ALU.add).then_inc(plus_done, 1)
                if g == 7:
                    dve.wait_ge(ln_done, ln.next())
                    nc.vector.scalar_tensor_tensor(UU[:], UU[:], -1.0, EX[:], ALU.add, ALU.subtract).then_inc(delta, 1)
                    dve.wait_ge(delta, dl.next())
                    nc.vector.tensor_tensor(DEL[:, q], DEL[:, q], UU[:], ALU.subtract).then_inc(delta, 1)
                    dve.wait_ge(delta, dl.next())
                    dve.wait_ge(relu_done, rlt.value())
                    nc.vector.tensor_tensor(DEL[:, q], DEL[:, q], DTX[:, q], ALU.add).then_inc(delta, 1)
                    dve.wait_ge(delta, dl.next())
                    nc.vector.tensor_tensor(DTX[:, q], DEL[:, q], XC[:, q], ALU.mult).then_inc(dtx_done, 1)

            def gate(q):
                accd.n += GR
                dve.wait_ge(acc_mm, accd.value())
                for h in range(DH):
                    nc.vector.scalar_tensor_tensor(YG[:, h, :], XC[:, q, h, :], vec[:, 6 + h:7 + h], PY[:, h, :], ALU.mult, ALU.add).then_inc(gated, 1)
                gt.n += 2
                dve.wait_ge(gated, gt.value())
                nc.vector.tensor_tensor(YG[:], YG[:], ZS[:, q], ALU.mult).then_inc(gated, 1)
                gt.n += 1

            def residual(n):
                dve.wait_ge(ot_done, otd.next())
                nc.vector.tensor_tensor(X[:, cols(n)], X[:, cols(n)], OT[:], ALU.add).then_inc(added, 1)
                addn.n += 1

            def chunk(i, q, back, more):
                dtxd.n += 1
                dve.wait_ge(dtx_done, dtxd.value())
                for g in range(GR):
                    dve.wait_ge(bb_mm, bbm.next())
                    dve.wait_ge(hc_done, hcf.next())
                    nc.vector.tensor_tensor(HB[:, g % 2], PB[:].unsqueeze(1).to_broadcast([128, DH, SG, CH]),
                                            DTX[:, q].unsqueeze(2).to_broadcast([128, DH, SG, CH]), ALU.mult).then_inc(b_done, 1)
                    dve.wait_ge(b_done, bd.next())
                    dve.wait_ge(da_done, da.next())
                    flat = lambda ap: ap.rearrange("p h k t -> p (h k t)")
                    nc.vector.tensor_tensor_scan(flat(HB[:, g % 2]), flat(DA[:, g % 2]), flat(HB[:, g % 2]), 0.0, ALU.mult, ALU.add).then_inc(scanned, 1)
                    if g == 1 and back:
                        gate(1 - q)
                    if g == 2 and back:
                        residual(i - 1)
                    if more:
                        front(i + 1, 1 - q, g)

            dtxd = Tally()
            for g in range(GR):
                front(0, 0, g)
            chunks(dve, chunk, [(mum, 1), (std_, 1), (dg, 2), (rsm, 1), (bcm, 1), (spl, 5), (abs_, DH), (rlt, DH), (ex, 1), (ln, 1), (dl, 3),
                                (bbm, GR), (hcf, GR), (bd, GR), (da, GR), (accd, GR), (gt, 3), (otd, 1), (addn, 1), (dtxd, 1)])
            gate(1)
            residual(NCH - 1)

        @block.gpsimd
        def _(pool):
            scn, cbd, accf = Tally(2), Tally(1), Tally(0)
            pool.wait_ge(zeroed, 6)

            def chunk(i, q, back, more):
                for g in range(GR):
                    pool.wait_ge(scanned, scn.next())
                    pool.wait_ge(cb_done, cbd.next())
                    pool.wait_ge(acc_mm, accf.next())
                    nc.gpsimd.tensor_tensor(HC[:, g % 2], HB[:, g % 2], CB[:, g % 2].unsqueeze(1).to_broadcast([128, DH, SG, CH]), ALU.mult).then_inc(hc_done, 1)

            chunks(pool, chunk, [(scn, GR), (cbd, GR), (accf, GR)])


H3 = 8
HC3 = C // H3
TILES = CH // 128


def linear_attention(nc, d, X, out):
    with ExitStack() as ctx:
        sem = lambda n: ctx.enter_context(nc.semaphore(n))
        sb = lambda n, s, dt=F32: ctx.enter_context(nc.sbuf_tensor(n, s, dt))
        kvw, qw, o1, o2, mask, ident = sb("kv_w", [128, 256]), sb("q_w3", [128, 128]), sb("o1_w", [128, 128]), sb("o2_w", [128, 128]), sb("kv_mask", [128, 128]), sb("ident3", [128, 128])
        lnw, lnb = sb("ln3_w", [128, 256]), sb("ln3_b", [128, 256])
        G = sb("o1_map", [128, B, 128])
        l3_in = sem("l3_in")
        with ExitStack() as c1:
            sb1 = lambda n, s, dt=F32: c1.enter_context(nc.sbuf_tensor(n, s, dt))
            XB = sb1("x_batch3", [128, HW])
            SQ, KV = sb1("kv_sq", [128, 2, TILES * 256]), sb1("kv_norm", [128, 3, TILES * 256])
            st = sb1("kv_std", [128, 2, TILES * 16])
            wm = sb1("w_mean", [128, 16])
            kvm, ai = sb1("kv_masked", [128, 128]), sb1("att_map", [128, 128])
            PS = c1.enter_context(nc.psum_tensor("kv_ps", [128, 2, TILES * 256], F32))
            ACC = c1.enter_context(nc.psum_tensor("kv_acc", [128, 512], F32))
            MAP = c1.enter_context(nc.psum_tensor("map_ps", [128, 512], F32))
            xb_ready, kv_mm, sq_done, ss_done, std_done, std_step, scaled, shifted, acc_mm, kvm_done, ai_mm, ai_done, g_mm, g_done, w_step = (
                sem("l3_" + n) for n in ("xb_ready", "kv_mm", "sq_done", "ss_done", "std_done", "std_step", "scaled", "shifted", "acc_mm",
                                         "kvm_done", "ai_mm", "ai_done", "g_mm", "g_done", "w_step"))
            norm_done = sem("l3_norm_done")
            block = c1.enter_context(nc.Block())

            @block.sync
            def _(sp):
                for dst, name in ((kvw, "l3_kvw"), (qw, "l3_qw"), (o1, "l3_o1"), (o2, "l3_o2"), (mask, "l3_mask"), (ident, "ident"),
                                  (lnw, "l3_lnw"), (lnb, "l3_lnb")):
                    sp.dma_start(dst[:], d[name]).then_inc(l3_in, 16)

            @block.tensor
            def _(pe):
                xb, sc, sh, gd, kd, ad = Tally(), Tally(), Tally(), Tally(), Tally(), Tally()
                pe.wait_ge(w_step, 3)

                def project(k):
                    if k >= 2:
                        pe.wait_ge(norm_done, sc.next())
                    for i in range(TILES):
                        e = k * TILES + i
                        m = nc.tensor.matmul(PS[:, k % 2, i * 256:(i + 1) * 256], XB[:, e * 128:(e + 1) * 128], kvw[:], start=True, stop=True)
                    m.then_inc(kv_mm, 1)

                def outer(k):
                    pe.wait_ge(shifted, sh.next())
                    for i in range(TILES):
                        m = nc.tensor.matmul(ACC[:, 0:128], KV[:, k % 3, i * 256:i * 256 + 128], KV[:, k % 3, i * 256 + 128:(i + 1) * 256],
                                             start=(k == 0 and i == 0), stop=(k == CPB - 1 and i == TILES - 1))
                    m.then_inc(acc_mm, 1)

                with counted_loop(pe, B, (xb, 1), (sc, CPB), (sh, CPB), (kd, 1), (ad, 1)) as b:
                    pe.wait_ge(xb_ready, xb.next())
                    for k in range(CPB):
                        project(k)
                        if k >= 1:
                            outer(k - 1)
                    outer(CPB - 1)
                    sc.n += 2
                    pe.wait_ge(kvm_done, kd.next())
                    nc.tensor.matmul(MAP[:, 0:128], kvm[:], qw[:], start=True, stop=True).then_inc(ai_mm, 1)
                    pe.wait_ge(ai_done, ad.next())
                    nc.tensor.matmul(MAP[:, 128:256], ai[:], o1[:], start=True, stop=True).then_inc(g_mm, 1)

            @block.scalar
            def _(act):
                mm, ss, st_ = Tally(), Tally(), Tally()
                sqf = Tally()
                act.wait_ge(l3_in, 16 * 8)

                with counted_loop(act, B, (mm, CPB), (ss, CPB), (sqf, CPB)) as b:
                    for k in range(CPB):
                        act.wait_ge(kv_mm, mm.next())
                        act.wait_ge(ss_done, sqf.next(0))
                        nc.scalar.activation(SQ[:, k % 2, :], PS[:, k % 2, :], ACT.Square).then_inc(sq_done, 1)
                        act.wait_ge(ss_done, ss.next(2))
                        nc.scalar.activation(st[:, k % 2, :], st[:, k % 2, :], ACT.Sqrt, scale=1.0 / (HC3 - 1)).then_inc(std_done, 1)

            @block.vector
            def _(dve):
                dve.wait_ge(l3_in, 16 * 8)
                g3 = kvw[:].rearrange("p (g c) -> p g c", c=HC3)
                nc.vector.tensor_reduce(wm[:], g3, AX.X, ALU.add).then_inc(w_step, 1)
                dve.wait_ge(w_step, 1)
                nc.vector.tensor_scalar(wm[:], wm[:], 1.0 / HC3, None, ALU.mult).then_inc(w_step, 1)
                dve.wait_ge(w_step, 2)
                nc.vector.tensor_tensor(g3, g3, wm[:].unsqueeze(2).to_broadcast([128, 16, HC3]), ALU.subtract).then_inc(w_step, 1)
                for s, k in ((ss_done, 2), (acc_mm, 3)):
                    nc.vector.memset(st[:, 0, 0:1], 0.0).then_inc(s, k)
                    dve.wait_ge(s, k)
                sq, sd, stp, nd, am, amm, gm, aim, gmm = (Tally() for _ in range(9))
                accf = Tally()
                with counted_loop(dve, B, (sq, CPB), (sd, CPB), (stp, 2 * CPB), (nd, CPB), (accf, CPB), (am, CPB), (aim, 1), (gmm, 1)) as b:
                    nc.vector.tensor_copy(XB[:], X[:, bass.ds(b * HW, HW)]).then_inc(xb_ready, 1)
                    for k in range(CPB):
                        dve.wait_ge(sq_done, sq.next())
                        nc.vector.tensor_reduce(st[:, k % 2, :], SQ[:, k % 2, :].rearrange("p (g c) -> p g c", c=HC3), AX.X, ALU.add).then_inc(ss_done, 1)
                        dve.wait_ge(std_done, sd.next())
                        nc.vector.tensor_scalar(st[:, k % 2, :], st[:, k % 2, :], 1e-5, None, ALU.add).then_inc(std_step, 1)
                        dve.wait_ge(std_step, stp.next())
                        nc.vector.reciprocal(st[:, k % 2, :], st[:, k % 2, :]).then_inc(std_step, 1)
                        dve.wait_ge(std_step, stp.next())
                        dve.wait_ge(acc_mm, accf.next())
                        nc.vector.tensor_tensor(KV[:, k % 3, :].rearrange("p (g c) -> p g c", c=HC3), PS[:, k % 2, :].rearrange("p (g c) -> p g c", c=HC3),
                                                st[:, k % 2, :].unsqueeze(2).to_broadcast([128, TILES * 16, HC3]), ALU.mult).then_inc(norm_done, 1)
                        dve.wait_ge(norm_done, nd.next())
                        kv4 = KV[:, k % 3, :].rearrange("p (t c) -> p t c", t=TILES)
                        nc.vector.tensor_tensor(kv4, kv4, lnw[:].unsqueeze(1).to_broadcast([128, TILES, 256]), ALU.mult).then_inc(scaled, 1)
                    am.n += CPB
                    dve.wait_ge(acc_mm, am.value(3))
                    nc.vector.tensor_tensor(kvm[:], ACC[:, 0:128], mask[:], ALU.mult).then_inc(kvm_done, 1)
                    dve.wait_ge(ai_mm, aim.next())
                    nc.vector.tensor_tensor(ai[:], MAP[:, 0:128], ident[:], ALU.add).then_inc(ai_done, 1)
                    dve.wait_ge(g_mm, gmm.next())
                    nc.vector.tensor_copy(G[:, bass.ds(b, 1), :], MAP[:, 128:256].rearrange("p (a c) -> p a c", a=1)).then_inc(g_done, 1)

            @block.gpsimd
            def _(pool):
                sc = Tally()
                pool.wait_ge(l3_in, 16 * 8)
                with counted_loop(pool, B, (sc, CPB)) as b:
                    for k in range(CPB):
                        pool.wait_ge(scaled, sc.next())
                        kv4 = KV[:, k % 3, :].rearrange("p (t c) -> p t c", t=TILES)
                        nc.gpsimd.tensor_tensor(kv4, kv4, lnb[:].unsqueeze(1).to_broadcast([128, TILES, 256]), ALU.add).then_inc(shifted, 1)

        U, R, O = sb("gelu_in", [128, 2, CH]), sb("mlp_sum", [128, 2, CH]), sb("out_tile", [128, 4, CH])
        PU, PO = ctx.enter_context(nc.psum_tensor("u_ps", [128, 2, CH], F32)), ctx.enter_context(nc.psum_tensor("o_ps", [128, 2, CH], F32))
        u_mm, u_done, o_mm, r_done, out_done = (sem("mlp_" + n) for n in ("u_mm", "u_done", "o_mm", "r_done", "out_done"))
        stored = [sem(f"mlp_stored{i}") for i in range(4)]
        block = ctx.enter_context(nc.Block())
        NC = B * CPB

        @block.tensor
        def _(pe):
            for n in range(NC + 1):
                if n < NC:
                    if n >= 2:
                        pe.wait_ge(u_done, n - 1)
                    nc.tensor.matmul(PU[:, n % 2, :], G[:, n // CPB, :], X[:, n * CH:(n + 1) * CH], start=True, stop=True).then_inc(u_mm, 1)
                if n >= 1:
                    pe.wait_ge(u_done, n)
                    if n >= 3:
                        pe.wait_ge(r_done, n - 2)
                    nc.tensor.matmul(PO[:, (n - 1) % 2, :], o2[:], U[:, (n - 1) % 2, :], start=True, stop=True).then_inc(o_mm, 1)

        @block.scalar
        def _(act):
            for n in range(NC + 2):
                if n < NC:
                    act.wait_ge(u_mm, n + 1)
                    if n >= 2:
                        act.wait_ge(o_mm, n - 1)
                    nc.scalar.activation(U[:, n % 2, :], PU[:, n % 2, :], ACT.Gelu).then_inc(u_done, 1)
                if n >= 2:
                    k = n - 2
                    act.wait_ge(r_done, k + 1)
                    if k >= 4:
                        act.wait_ge(stored[k % 4], 16 * (k // 4))
                    nc.scalar.activation(O[:, k % 4, :], R[:, k % 2, :], ACT.Gelu).then_inc(out_done, 1)

        @block.vector
        def _(dve):
            for n in range(NC):
                dve.wait_ge(o_mm, n + 1)
                if n >= 2:
                    dve.wait_ge(out_done, n - 1)
                nc.vector.tensor_tensor(R[:, n % 2, :], PO[:, n % 2, :], X[:, n * CH:(n + 1) * CH], ALU.add).then_inc(r_done, 1)

        @block.sync
        def _(sp):
            for n in range(NC):
                sp.wait_ge(out_done, n + 1)
                sp.dma_start(out[:, n // CPB, (n % CPB) * CH:(n % CPB + 1) * CH], O[:, n % 4, :]).then_inc(stored[n % 4], 16)
            for i in range(4):
                sp.wait_ge(stored[i], 16 * (NC // 4))


class Kept:
    pass


def program(nc, d, out):
    with ExitStack() as ctx:
        X = ctx.enter_context(nc.sbuf_tensor("x_all", [128, N], F32))
        with ExitStack() as l0:
            sb = lambda n, s, dt=F32: l0.enter_context(nc.sbuf_tensor(n, s, dt))
            t = Kept()
            t.qk_w = sb("qk_w", [128, HEADS, 2, 96])
            t.qk_full = sb("qk_full", [128, 256])
            t.v_w = sb("v_w", [128, 128])
            t.proj_w = sb("proj_w", [128, 128])
            t.qk_b = sb("qk_b", [96, 2 * HEADS])
            t.ident = sb("ident", [128, 128])
            t.ident16 = sb("ident16", [128, 128], F16)
            t.sel = sb("sel", [97, 2, HD])
            t.qk_scale = sb("qk_scale", [128, 4])
            t.out_b = sb("out_b", [128, 1])
            setup_attention(nc, d, X, t)
            attention(nc, X, t)
        binary_conv(nc, d, X)
        mamba(nc, d, X)
        linear_attention(nc, d, X, out)


def more_arrays(arrays, g, col, np):
    w1 = g("L1_conv_w")
    arrays["l1_wt"] = w1.transpose(1, 2, 3, 0).reshape(C, TAPS * C)
    arrays["l1_wr"] = w1.reshape(C, C * TAPS)
    arrays["l1_vec"] = np.concatenate([col(g("L1_conv_" + n)) for n in ("bias0", "gamma", "beta", "bias1", "alpha", "bias2")], axis=1)
    two = lambda a: np.reshape(a, (DH, 128, -1)).transpose(1, 0, 2)
    wx = g("L2_conv_W_x")
    arrays["l2_w_in"] = g("L2_conv_W_in")
    arrays["l2_w_out"] = two(g("L2_conv_W_out"))
    arrays["l2_w_bc"] = np.tile(two(wx[:, DTR:]), (1, 1, 3))
    arrays["l2_wdr"] = wx[:, :DTR].T
    arrays["l2_dtw"] = g("L2_conv_dt_w")
    arrays["l2_alog"] = two(g("L2_conv_A_log")).reshape(128, DH * NS)
    halves = lambda n: two(g("L2_conv_" + n)).reshape(128, -1)
    b_in = np.reshape(g("L2_conv_b_in"), (4, 128)).T
    arrays["l2_vec"] = np.concatenate([col(g("L2_conv_b_out")), col(g("L2_conv_b_out")), halves("conv_b"), halves("dt_b"), halves("D"), b_in,
                                       col(g("L2_conv_ln_g")), col(g("L2_conv_ln_b")), halves("conv_w")], axis=1)
    arrays["l2_onehot"] = np.tile(np.eye(2 * NS, dtype=np.float32), (3, 1))
    w3 = np.reshape(g("L3_conv_qkv_w"), (H3, 3, HC3, C))
    arrays["l3_qw"] = w3[:, 0].reshape(C, C)
    arrays["l3_kvw"] = w3[:, 1:3].transpose(3, 1, 0, 2).reshape(C, 2 * C)
    arrays["l3_o1"] = g("L3_conv_o1_w").T
    arrays["l3_o2"] = g("L3_conv_o2_w").T
    for n in "wb":
        kn, vn = g("L3_conv_kln_" + n), g("L3_conv_vln_" + n)
        arrays["l3_ln" + n] = np.tile(np.concatenate([np.reshape(kn, (1, C)), np.reshape(vn, (1, C))], axis=1), (128, 1))
    arrays["l3_mask"] = np.kron(np.eye(H3), np.full((HC3, HC3), 1.0 / HW)).astype(np.float32)


def kernel(**inputs):
    import numpy as np
    import concourse.bacc as bacc
    from concourse.bass_utils import run_bass_kernel_spmd

    g = lambda n: np.asarray(inputs[n])
    col = lambda a: np.reshape(a, (-1, 1))
    arrays = {}
    arrays["x"] = np.reshape(g("x"), (B, C, HW)).transpose(1, 0, 2)
    w, wb = g("L0_conv_qkv_w"), g("L0_conv_qkv_b")
    wq = np.reshape(w[:2 * C], (2, HEADS, HD, C)).transpose(3, 1, 0, 2)
    arrays["qk_w"] = np.tile(wq[:, :, :, None, :], (1, 1, 1, 3, 1)).reshape(C, HEADS, 2, 3 * HD)
    bq = np.reshape(wb[:2 * C], (2, HEADS, HD)).transpose(2, 1, 0)
    arrays["qk_b"] = np.tile(bq[None], (3, 1, 1, 1)).reshape(3 * HD, 2 * HEADS)
    arrays["qk_full"] = w[:2 * C].T
    arrays["v_w"] = w[2 * C:].T
    arrays["proj_w"] = g("L0_conv_proj_w").T
    arrays["l0_vec"] = np.concatenate([col(g("L0_conv_gn_w")), col(g("L0_conv_gn_b")), col(wb[2 * C:]), col(g("L0_conv_proj_b")),
                                       col(wb[:C]), col(wb[C:2 * C]), col(wb[:C]), col(wb[:C])], axis=1)
    cg = C // GROUPS
    arrays["group_avg"] = np.kron(np.eye(GROUPS), np.full((cg, cg), 1.0 / cg)).astype(np.float32)
    arrays["ones_row"] = np.ones((1, 128), np.float32)
    arrays["ident"] = np.eye(128, dtype=np.float32)
    sel = np.zeros((97, 2, HD), np.float32)
    for half in (0, 64):
        sel[half:half + HD, 0, :] = np.eye(HD)
        sel[half + HD, 1, :] = 1.0
    arrays["sel"] = sel
    more_arrays(arrays, g, col, np)

    nc = bacc.Bacc("TRN2", target_bir_lowering=False, num_devices=1)
    d = {}
    for name in arrays:
        arrays[name] = np.ascontiguousarray(arrays[name])
        d[name] = nc.dram_tensor("in_" + name, arrays[name].shape, mybir.dt.from_np(arrays[name].dtype), kind="ExternalInput").ap()
    out = nc.dram_tensor("out", (B, C, HW), F32, kind="ExternalOutput").ap()
    program(nc, d, out.rearrange("b c n -> c b n"))
    r = run_bass_kernel_spmd(nc, [{"in_" + k: v for k, v in arrays.items()}], core_ids=[0])
    return np.reshape(r.results[0]["out"], (B, C, H, W))
```

```python
from contextlib import ExitStack, contextmanager

import concourse.bass as bass
from concourse import mybir

F32 = mybir.dt.float32
F16 = mybir.dt.float16
BF16 = mybir.dt.bfloat16
ALU = mybir.AluOpType
ACT = mybir.ActivationFunctionType
AX = mybir.AxisListType

B, C, H, W = 4, 128, 64, 64
HW = H * W
N = B * HW
CH = 512
CPB = HW // CH


class Tally:

    def __init__(self, primed=0):
        self.n = primed
        self.loops = []

    def value(self, ahead=0):
        v = self.n + ahead
        for term in self.loops:
            v = term + v
        return v

    def next(self, ahead=0):
        self.n += 1
        return self.value(ahead)


@contextmanager
def counted_loop(eng, count, *tallies):
    before = [t.n for t, _ in tallies]
    with eng.Fori(0, count) as i:
        for t, k in tallies:
            t.loops.append(i * k)
        yield i
        for (t, k), n in zip(tallies, before):
            assert t.n - n == k, (t.n - n, k)
    for (t, k), n in zip(tallies, before):
        t.loops.pop()
        t.n = n + count * k


class Chain:

    def __init__(self, eng, sem):
        self.eng, self.sem, self.done = eng, sem, Tally()

    def step(self, ins):
        ins.then_inc(self.sem, 1)
        self.eng.wait_ge(self.sem, self.done.next())
GROUPS = 8
HEADS = 4
HD = C // HEADS
ET = HW // 128
PAIRS = ET // 2
DT = CH // 128
ABLK = DT * CPB
QBOUND = 4096.0
MROW = 32768.0


def setup_attention(nc, d, X, t):
    with ExitStack() as ctx:
        sem = lambda n: ctx.enter_context(nc.semaphore(n))
        sb = lambda n, s, dt=F32: ctx.enter_context(nc.sbuf_tensor(n, s, dt))
        ps = ctx.enter_context(nc.psum_tensor("setup_ps", [128, 512], F32))
        x_in = [sem(f"x_in{b}") for b in range(B)]
        const_in, dve_step, pe_step, act_step = sem("const_in"), sem("su_dve"), sem("su_pe"), sem("su_act")
        stats = sb("gn_stats", [128, B, CPB, 6])
        cst = sb("gn_channel", [128, B, 2])
        grp = sb("gn_group", [128, 8, B])
        vec = sb("l0_vec", [128, 8])
        group_avg = sb("group_avg", [128, 128])
        ones_row = sb("ones_row", [1, 128])
        absw = sb("absw", [128, 256])
        bnd = sb("bnd", [128, 4])
        row = sb("bnd_row", [1, 256])
        top = sb("bnd_top", [1, 2])
        block = ctx.enter_context(nc.Block())
        loads = [(t.qk_w, d["qk_w"]), (t.v_w, d["v_w"]), (t.proj_w, d["proj_w"]), (vec, d["l0_vec"]),
                 (t.qk_b, d["qk_b"]), (group_avg, d["group_avg"]), (ones_row, d["ones_row"]), (t.ident, d["ident"]),
                 (t.sel, d["sel"]), (t.ones, d["ones"]), (t.qk_full, d["qk_full"])]

        @block.sync
        def _(sp):
            for b in range(B):
                sp.dma_start(X[:, b * HW:(b + 1) * HW], d["x"][:, b, :]).then_inc(x_in[b], 16)

        @block.scalar
        def _(act):
            for dst, src in loads:
                act.dma_start(dst[:], src).then_inc(const_in, 16)
            act.wait_ge(dve_step, V_VAR)
            nc.scalar.activation(grp[:, 5, :], grp[:, 4, :], ACT.Sqrt).then_inc(act_step, 1)

        @block.vector
        def _(dve):
            ch = Chain(dve, dve_step)
            for b in range(B):
                dve.wait_ge(x_in[b], 16)
                for k in range(CPB):
                    nc.vector.bn_stats(stats[:, b, k, :], X[:, b * HW + k * CH: b * HW + (k + 1) * CH]).then_inc(dve_step, 1)
                    ch.done.n += 1
                dve.wait_ge(dve_step, ch.done.value())
                ch.step(nc.vector.bn_aggr(cst[:, b, :], stats[:, b, :, :].rearrange("p k s -> p (k s)")))
            assert ch.done.n == V_STAT, ch.done.n
            dve.wait_ge(const_in, 16 * len(loads))
            dve.wait_ge(pe_step, 1)
            ch.step(nc.vector.tensor_copy(grp[:, 0, :], ps[:, 0:B]))
            ch.step(nc.vector.tensor_tensor(grp[:, 1, :], cst[:, :, 0], grp[:, 0, :], ALU.subtract))
            ch.step(nc.vector.tensor_tensor(grp[:, 2, :], grp[:, 1, :], grp[:, 1, :], ALU.mult))
            ch.step(nc.vector.tensor_tensor(grp[:, 3, :], grp[:, 2, :], cst[:, :, 1], ALU.add))
            assert ch.done.n == V_DEV, ch.done.n
            dve.wait_ge(pe_step, 2)
            ch.step(nc.vector.tensor_scalar(grp[:, 4, :], ps[:, B:2 * B], 1e-5, None, ALU.add))
            assert ch.done.n == V_VAR, ch.done.n
            dve.wait_ge(act_step, 1)
            ch.step(nc.vector.reciprocal(grp[:, 6, :], grp[:, 5, :]))
            ch.step(nc.vector.tensor_scalar(grp[:, 6, :], grp[:, 6, :], vec[:, 0:1], None, ALU.mult))
            ch.step(nc.vector.tensor_tensor(grp[:, 7, :], grp[:, 0, :], grp[:, 6, :], ALU.mult))
            ch.step(nc.vector.tensor_scalar(grp[:, 7, :], grp[:, 7, :], -1.0, vec[:, 1:2], ALU.mult, ALU.add))
            for b in range(B):
                xb = X[:, b * HW:(b + 1) * HW]
                nc.vector.tensor_scalar(xb, xb, grp[:, 6, b:b + 1], grp[:, 7, b:b + 1], ALU.mult, ALU.add).then_inc(dve_step, 1)
                ch.done.n += 1
            ch.step(nc.vector.tensor_scalar(absw[:], t.qk_full[:], -1.0, None, ALU.mult))
            ch.step(nc.vector.tensor_tensor(absw[:], absw[:], t.qk_full[:], ALU.max))
            ch.step(nc.vector.tensor_scalar(vec[:, 6:8], vec[:, 0:2], -1.0, None, ALU.mult))
            ch.step(nc.vector.tensor_tensor(vec[:, 6:8], vec[:, 6:8], vec[:, 0:2], ALU.max))
            ch.step(nc.vector.scalar_tensor_tensor(vec[:, 6:7], vec[:, 6:7], float(HW * C // GROUPS) ** 0.5, vec[:, 7:8], ALU.mult, ALU.add))
            assert ch.done.n == V_ABS, ch.done.n
            ch.step(nc.vector.tensor_scalar(bnd[:, 0:2], vec[:, 4:6], -1.0, None, ALU.mult))
            ch.step(nc.vector.tensor_tensor(bnd[:, 0:2], bnd[:, 0:2], vec[:, 4:6], ALU.max))
            dve.wait_ge(pe_step, 3)
            ch.step(nc.vector.tensor_tensor(bnd[:, 2:4], ps[:, 8:10], bnd[:, 0:2], ALU.add))
            assert ch.done.n == V_BND, ch.done.n
            dve.wait_ge(pe_step, 4)
            ch.step(nc.vector.tensor_copy(row[:], ps[0:1, 16:272]))
            ch.step(nc.vector.tensor_reduce(top[:, 0:1], row[:], AX.X, ALU.max))
            ch.step(nc.vector.tensor_scalar(top[:, 1:2], top[:, 0:1], 1e-3, 1.0 / QBOUND, ALU.max, ALU.mult))
            assert ch.done.n == V_TOP, ch.done.n
            dve.wait_ge(pe_step, 5)
            ch.step(nc.vector.tensor_copy(t.qk_scale[:, 2:3], ps[:, 300:301]))
            ch.step(nc.vector.reciprocal(t.qk_scale[:, 0:1], t.qk_scale[:, 2:3]))
            ch.step(nc.vector.tensor_scalar(t.qk_scale[:, 1:2], t.qk_scale[:, 2:3], t.qk_scale[:, 2:3], float(C) ** -0.5, ALU.mult, ALU.mult))
            ch.step(nc.vector.tensor_scalar(t.qk_b[:], t.qk_b[:], t.qk_scale[0:96, 0:1], None, ALU.mult))
            dve.wait_ge(pe_step, 6)
            ch.step(nc.vector.tensor_tensor(t.out_b[:, 0:1], ps[:, 304:305], vec[:, 3:4], ALU.add))
            ch.step(nc.vector.tensor_copy(t.ident16[:], t.ident[:]))

        @block.tensor
        def _(pe):
            pe.wait_ge(const_in, 16 * len(loads))
            pe.wait_ge(dve_step, V_STAT)
            nc.tensor.matmul(ps[:, 0:B], group_avg[:], cst[:, :, 0], start=True, stop=True).then_inc(pe_step, 1)
            pe.wait_ge(dve_step, V_DEV)
            nc.tensor.matmul(ps[:, B:2 * B], group_avg[:], grp[:, 3, :], start=True, stop=True).then_inc(pe_step, 1)
            pe.wait_ge(dve_step, V_ABS)
            nc.tensor.matmul(ps[:, 8:9], absw[:, 0:128], vec[:, 6:7], start=True, stop=True)
            nc.tensor.matmul(ps[:, 9:10], absw[:, 128:256], vec[:, 6:7], start=True, stop=True).then_inc(pe_step, 1)
            pe.wait_ge(dve_step, V_BND)
            nc.tensor.matmul(ps[0:1, 16:144], bnd[:, 2:3], t.ident[:], start=True, stop=True)
            nc.tensor.matmul(ps[0:1, 144:272], bnd[:, 3:4], t.ident[:], start=True, stop=True).then_inc(pe_step, 1)
            pe.wait_ge(dve_step, V_TOP)
            nc.tensor.matmul(ps[:, 300:301], ones_row[:], top[:, 1:2], start=True, stop=True).then_inc(pe_step, 1)
            pe.wait_ge(dve_step, V_TOP + 1)
            nc.tensor.matmul(ps[:, 304:305], t.proj_w[:], vec[:, 2:3], start=True, stop=True).then_inc(pe_step, 1)


V_STAT = B * (CPB + 1)
V_DEV = V_STAT + 4
V_VAR = V_DEV + 1
V_ABS = V_VAR + 4 + B + 5
V_BND = V_ABS + 3
V_TOP = V_BND + 3


def attention(nc, X, t):
    with ExitStack() as ctx:
        sem = lambda n: ctx.enter_context(nc.semaphore(n))
        sb = lambda n, s, dt=F32: ctx.enter_context(nc.sbuf_tensor(n, s, dt))
        pst = lambda n, s: ctx.enter_context(nc.psum_tensor(n, s, F32))
        XB = sb("xn_batch", [128, HW])
        QS = [sb(f"q_stack{i}", [128, HW], F16) for i in range(2)]
        KS = [sb(f"k_stack{i}", [128, HW], F16) for i in range(2)]
        VS, VN = sb("v_ones", [128, HEADS, ET, HD + 1]), sb("v_next", [128, HEADS, ET, HD + 1])
        QK32 = sb("qk32", [96, 2, CH])
        P = sb("probs", [128, 4, 2, CH])
        AO = sb("att_out", [128, HW])
        OS = sb("out_sums", [128, CH])
        RS, RD = sb("recip_rows", [128, CH]), sb("recip_diag", [128, DT, 128])
        R4 = sb("recip", [128, DT])
        M8 = sb("block_max", [128, DT, CPB])
        M4 = sb("row_max", [128, DT])
        MC = sb("max_cols", [128, DT, 2], F16)
        S, A, O, M = pst("scores", [128, 4, CH]), pst("ring", [128, 2, CH]), pst("out_acc", [128, CH]), pst("misc", [128, CH])

        xb_ready, ready, v_ready = sem("xb_ready"), sem("l0_ready"), sem("v_ready")
        ring_mm, ring_free, split_done = sem("ring_mm"), sem("ring_free"), sem("split_done")
        m_step, m_cols, m_rows, m_ready = sem("m_step"), sem("m_cols"), sem("m_rows"), sem("m_ready")
        b_mm, exp_done, pv_done, o_copied = sem("b_mm"), sem("exp_done"), sem("pv_done"), sem("o_copied")
        den_mm, den_step, rb_mm, rb_copied, num_mm, ao_done = sem("den_mm"), sem("den_step"), sem("rb_mm"), sem("rb_copied"), sem("num_mm"), sem("ao_done")
        pj_mm, pj_done = sem("pj_mm"), sem("pj_done")
        block = ctx.enter_context(nc.Block())
        LAST = CPB - 1
        cols = lambda c: bass.ds(c * CH, CH)
        rows = lambda h: slice(HD * h, HD * h + HD)

        def ring(h, c, more):
            at = [[] for _ in range(PAIRS)]
            follows = h < HEADS - 1 or more
            prep = [("prep", 0), ("prep", 1)] if follows else []
            peak = [("max", n) for n in range(ABLK)] if c < LAST or follows else []
            vals = [("v", g) for g in range(ET // 4)] if (h, c) == (HEADS - 1, 0) and more else []
            if c < LAST:
                todo, first = vals + peak, 0
                for where, p in zip((6, 18), prep):
                    todo.insert(where, p)
            else:
                at[0] += prep
                todo, first = peak, 2
            span = PAIRS - 2 - first
            for i, what in enumerate(todo):
                at[first + i * span // len(todo)].append(what)
            return at

        ringed = lambda h, c, more: sum(len(x) for x in ring(h, c, more))
        RING = sum(ringed(h, c, True) for h in range(HEADS) for c in range(CPB))
        CHUNKS = HEADS * CPB
        DEN, RB, NUM, PROJ, ROWS_AT = 2, 4, 6, 8, PAIRS - 1

        def batches(eng, batch, tallies):
            with counted_loop(eng, B - 1, *tallies) as b:
                batch(b, True)
            batch(B - 1, False)

        def heads(eng, chunk, more, tallies):
            for h in range(HEADS):
                chunk(h, 0, (h - 1, LAST) if h > 0 else None)
                with counted_loop(eng, LAST - 1, *tallies(h)) as turn:
                    chunk(h, turn + 1, (h, turn))
                chunk(h, LAST, (h, LAST - 1))

        @block.gpsimd
        def _(pool):
            for i, (what, v) in enumerate(((VN[:, :, :, HD:HD + 1], 1.0), (KS[0][96:128, :], MROW), (KS[1][96:128, :], MROW), (OS[:], 1.0))):
                nc.gpsimd.memset(what, v).then_inc(ready, 1)
                pool.wait_ge(ready, i + 1)

        @block.vector
        def _(dve):
            for s, k in ((ring_free, 2), (exp_done, 2), (pv_done, 4), (o_copied, 1), (pj_done, 1)):
                nc.vector.memset(R4[:, 0:1], 0.0).then_inc(s, k)
                dve.wait_ge(s, k)
            dve.wait_ge(ready, 4)
            rmm, rfr, split = Tally(), Tally(2), Tally()
            ms, mr, dm, ds_, nm, pj, pjd = Tally(), Tally(), Tally(), Tally(), Tally(), Tally(), Tally()

            def entry(what, nh, nc_, c):
                kind, n = what
                bank = A[:, rmm.n % 2, :]
                dve.wait_ge(ring_mm, rmm.next())
                if kind == "max":
                    nc.vector.reduce_max(M8[:, n // CPB, n % CPB:n % CPB + 1], bank, AX.X).then_inc(ring_free, 1)
                elif kind == "v":
                    nc.vector.tensor_copy(VN[:, :, 4 * n:4 * n + 4, 0:HD].rearrange("p h t c -> p t h c"),
                                          bank.rearrange("p (t h c) -> p t h c", t=4, h=HEADS)).then_inc(ring_free, 1)
                else:
                    st, lo = ((QS, slice(32, 64)), (KS, slice(64, 96)))[n]
                    st = st[c[0] % 2]
                    nc.vector.tensor_scalar(QK32[:, n, :], bank[0:96], t.qk_scale[0:96, 0:1], t.qk_b[:, 2 * c[0] + n:2 * c[0] + n + 1],
                                            ALU.mult, ALU.add).then_inc(ring_free, 1)
                    dve.wait_ge(ring_free, rfr.value(1))
                    nc.vector.tensor_copy(st[0:96, cols(c[1])], QK32[:, n, :]).then_inc(split_done, 1)
                    dve.wait_ge(split_done, split.next())
                    nc.vector.tensor_tensor(st[lo, cols(c[1])], QK32[lo, n, :], st[lo, cols(c[1])], ALU.subtract).then_inc(split_done, 1)
                    dve.wait_ge(split_done, split.next())
                rfr.n += 1

            def row_max(nh, nc_):
                dve.wait_ge(ring_free, rfr.value())
                nc.vector.reduce_max(M4[:], M8[:], AX.X).then_inc(m_step, 1)
                dve.wait_ge(m_step, ms.next())
                nc.vector.tensor_scalar(MC[:, :, 0], M4[:], -1.0 / MROW, None, ALU.mult).then_inc(m_step, 1)
                dve.wait_ge(m_step, ms.next())
                nc.vector.scalar_tensor_tensor(MC[:, :, 1], M4[:], -1.0 / MROW, MC[:, :, 0], ALU.mult, ALU.subtract).then_inc(m_cols, 1)
                dve.wait_ge(m_rows, mr.next())
                nc.vector.tensor_copy(QS[nh % 2][96:98, cols(nc_)], M[96:98, :]).then_inc(m_ready, 1)

            def finish(j, b, h, c):
                if j == DEN:
                    dve.wait_ge(den_mm, dm.next())
                    nc.vector.reciprocal(R4[:], M[:, 0:DT]).then_inc(den_step, 1)
                    dve.wait_ge(den_step, ds_.next())
                    nc.vector.tensor_tensor(RD[:], t.ident[:].unsqueeze(1).to_broadcast([128, DT, 128]), R4[:].unsqueeze(2).to_broadcast([128, DT, 128]),
                                            ALU.mult).then_inc(den_step, 1)
                    ds_.n += 1
                if j == NUM:
                    dve.wait_ge(num_mm, nm.next())
                    nc.vector.tensor_tensor(AO[rows(h), cols(c)], M[rows(h), :], RS[rows(h), :], ALU.mult).then_inc(ao_done, 1)
                if j == PROJ and h == HEADS - 1:
                    dve.wait_ge(pj_mm, pj.next())
                    xc = X[:, bass.ds(b * HW + c * CH, CH)]
                    nc.vector.scalar_tensor_tensor(xc, M[:], t.out_b[:, 0:1], xc, ALU.add, ALU.add).then_inc(pj_done, 1)
                    pjd.n += 1

            def batch(b, more):
                def chunk(h, c, before):
                    at = ring(h, c if isinstance(c, int) else 1, more)
                    last = isinstance(c, int) and c == LAST
                    nxt = ((h + 1) % HEADS, 0) if last else (h, c + 1)
                    for j in range(PAIRS):
                        for what in at[j]:
                            entry(what, *nxt, ((h + 1) % HEADS, c))
                        if before:
                            finish(j, b, *before)
                        if j == ROWS_AT and (not last or h < HEADS - 1 or more):
                            row_max(*nxt)
                    if last and h == HEADS - 2 and more:
                        nc.vector.tensor_copy(XB[:], X[:, bass.ds((b + 1) * HW, HW)]).then_inc(xb_ready, 1)

                heads(dve, chunk, more, lambda h: [(rmm, ringed(h, 1, more)), (rfr, ringed(h, 1, more)), (split, 4 if h < HEADS - 1 or more else 0), (ms, 2), (mr, 1),
                                                   (dm, 1), (ds_, 2), (nm, 1), (pj, int(h == HEADS - 1)), (pjd, int(h == HEADS - 1))])
                for j in (DEN, NUM, PROJ):
                    finish(j, b, HEADS - 1, LAST)
                if more:
                    nc.vector.tensor_copy(VS[:], VN[:]).then_inc(v_ready, 1)

            nc.vector.tensor_copy(XB[:], X[:, 0:HW]).then_inc(xb_ready, 1)
            for g in range(ET // 4):
                entry(("v", g), 0, 0, None)
            for c in range(CPB):
                for n in range(2):
                    entry(("prep", n), 0, 0, (0, c))
            for n in range(ABLK):
                entry(("max", n), 0, 0, None)
            dve.wait_ge(ring_free, rfr.value())
            nc.vector.tensor_copy(VS[:], VN[:]).then_inc(v_ready, 1)
            row_max(0, 0)
            batches(dve, batch, [(rmm, RING), (rfr, RING), (split, 4 * CHUNKS), (ms, 2 * CHUNKS), (mr, CHUNKS), (dm, CHUNKS), (ds_, 2 * CHUNKS),
                                 (nm, CHUNKS), (pj, CPB), (pjd, CPB)])

        @block.scalar
        def _(act):
            act.wait_ge(ready, 4)
            bm, pv_free, rb, ofr = Tally(), Tally(), Tally(), Tally()

            def copy_sums():
                act.wait_ge(pv_done, ofr.next())
                nc.scalar.copy(OS[0:HD + 1, :], O[0:HD + 1, :])
                nc.scalar.copy(OS[64:64 + HD + 1, :], O[64:64 + HD + 1, :]).then_inc(o_copied, 1)

            def copy_recip(h):
                act.wait_ge(rb_mm, rb.next())
                nc.scalar.copy(RS[rows(h), :], M[rows(h), :]).then_inc(rb_copied, 1)

            def batch(b, more):
                def chunk(h, c, before):
                    for j in range(PAIRS):
                        act.wait_ge(b_mm, bm.next())
                        act.wait_ge(pv_done, pv_free.next())
                        nc.scalar.activation(P[:, j % 4, :, :], S[:, 2 * (j % 2):2 * (j % 2) + 2, :], ACT.Exp,
                                             scale=t.qk_scale[:, 1:2]).then_inc(exp_done, 1)
                        if before and j == 0:
                            act.wait_ge(pv_done, pv_free.value(3))
                            nc.scalar.copy(OS[0:HD + 1, :], O[0:HD + 1, :])
                            nc.scalar.copy(OS[64:64 + HD + 1, :], O[64:64 + HD + 1, :]).then_inc(o_copied, 1)
                        if before and j == RB:
                            copy_recip(before[0])

                heads(act, chunk, more, lambda h: [(bm, PAIRS), (pv_free, PAIRS), (rb, 1)])
                act.wait_ge(pv_done, pv_free.value(4))
                nc.scalar.copy(OS[0:HD + 1, :], O[0:HD + 1, :])
                nc.scalar.copy(OS[64:64 + HD + 1, :], O[64:64 + HD + 1, :]).then_inc(o_copied, 1)
                copy_recip(HEADS - 1)

            batches(act, batch, [(bm, PAIRS * CHUNKS), (pv_free, PAIRS * CHUNKS), (rb, CHUNKS)])

        @block.tensor
        def _(pe):
            pe.wait_ge(ready, 4)
            xb, vr, rfr, rix, spl, mc, mrd = Tally(), Tally(), Tally(), Tally(), Tally(), Tally(), Tally()
            exf, exd, ocf, oc, dsd, rbc, aod, pjd = Tally(), Tally(2), Tally(), Tally(1), Tally(), Tally(), Tally(), Tally(1)

            def entry(what, nh, nc_, c):
                kind, n = what
                bank = A[:, rfr.n % 2, :]
                pe.wait_ge(ring_free, rfr.next())
                if kind == "max":
                    m = nc.tensor.matmul(bank, QS[nh % 2][0:96, bass.ds(nc_ * CH + (n // CPB) * 128, 128)],
                                         KS[nh % 2][0:96, (n % CPB) * CH:(n % CPB + 1) * CH], start=True, stop=True)
                elif kind == "v":
                    for k in range(4):
                        e = 4 * n + k
                        m = nc.tensor.matmul(bank[:, k * 128:(k + 1) * 128], XB[:, e * 128:(e + 1) * 128], t.v_w[:], start=True, stop=True)
                else:
                    m = nc.tensor.matmul(bank[0:96], t.qk_w[:, c[0], n, :], XB[:, cols(c[1])], start=True, stop=True)
                    spl.n += 2
                m.then_inc(ring_mm, 1)

            def max_rows():
                pe.wait_ge(m_cols, mc.next())
                for k in range(DT):
                    m = nc.tensor.matmul(M[96:98, k * 128:(k + 1) * 128], MC[:, k, :], t.ident16[:], start=True, stop=True)
                m.then_inc(m_rows, 1)

            def pair_scores(h, c, j, i):
                if i == 0:
                    pe.wait_ge(exp_done, exf.next())
                e = 2 * j + i
                m = nc.tensor.matmul(S[:, 2 * (j % 2) + i, :], KS[h % 2][0:98, e * 128:(e + 1) * 128], QS[h % 2][0:98, cols(c)], start=True, stop=True)
                if i == 1:
                    m.then_inc(b_mm, 1)

            def pair_out(h, j, i):
                if i == 0:
                    pe.wait_ge(exp_done, exd.next())
                    if j == 0:
                        pe.wait_ge(o_copied, ocf.next())
                m = nc.tensor.matmul(O[64 * i:64 * i + HD + 1, :], VS[:, h, 2 * j + i, :], P[:, j % 4, i, :],
                                     start=(j == 0), stop=(j == PAIRS - 1))
                if i == 1:
                    m.then_inc(pv_done, 1)

            def finish(j, h, c):
                if j == DEN:
                    pe.wait_ge(o_copied, oc.next())
                    for k in range(DT):
                        m = nc.tensor.matmul(M[:, k:k + 1], OS[0:97, k * 128:(k + 1) * 128], t.sel[0:97, 1, 0:1], start=True, stop=True)
                    m.then_inc(den_mm, 1)
                if j == RB:
                    dsd.n += 2
                    pe.wait_ge(den_step, dsd.value())
                    nc.tensor.matmul(M[rows(h), :], t.ones[:, 0:HD], RD[:].rearrange("p k c -> p (k c)"), start=True, stop=True).then_inc(rb_mm, 1)
                if j == NUM:
                    pe.wait_ge(rb_copied, rbc.next())
                    nc.tensor.matmul(M[rows(h), :], t.sel[0:97, 0, :], OS[0:97, :], start=True, stop=True).then_inc(num_mm, 1)
                    aod.n += 1
                if j == PROJ and h == HEADS - 1:
                    pe.wait_ge(ao_done, aod.value())
                    nc.tensor.matmul(M[:], t.proj_w[:], AO[:, cols(c)], start=True, stop=True).then_inc(pj_mm, 1)
                    pjd.n += 1

            def batch(b, more):
                def chunk(h, c, before):
                    at = ring(h, c if isinstance(c, int) else 1, more)
                    last = isinstance(c, int) and c == LAST
                    nxt = ((h + 1) % HEADS, 0) if last else (h, c + 1)
                    pe.wait_ge(m_ready, mrd.next())
                    if h == HEADS - 1 and isinstance(c, int) and c == 0 and more:
                        pe.wait_ge(xb_ready, xb.next())
                    for j in range(PAIRS):
                        share = [at[j][k * len(at[j]) // 3:(k + 1) * len(at[j]) // 3] for k in range(3)]
                        if len(at[j]) == 2:
                            share = [at[j][:1], [], at[j][1:]]

                        def entries(k):
                            for what in share[k]:
                                if what == ("max", 0) and last:
                                    pe.wait_ge(split_done, spl.value())
                                entry(what, *nxt, ((h + 1) % HEADS, c))

                        out = (h, j - 1) if j >= 1 else (before[0], PAIRS - 1) if before else None
                        pair_scores(h, c, j, 0)
                        entries(0)
                        pair_scores(h, c, j, 1)
                        entries(1)
                        if j == ROWS_AT and (not last or h < HEADS - 1 or more):
                            if before:
                                pe.wait_ge(ao_done, aod.value())
                            if not before or before[0] == HEADS - 1:
                                pe.wait_ge(pj_done, pjd.value())
                            max_rows()
                        if out:
                            pair_out(*out, 0)
                            pair_out(*out, 1)
                        else:
                            pe.wait_ge(v_ready, vr.next())
                        entries(2)
                        if before:
                            finish(j, *before)

                heads(pe, chunk, more, lambda h: [(rfr, ringed(h, 1, more)), (spl, 4 if h < HEADS - 1 or more else 0), (mc, 1), (mrd, 1), (exf, PAIRS), (exd, PAIRS),
                                                  (ocf, 1), (oc, 1), (dsd, 2), (rbc, 1), (aod, 1), (pjd, int(h == HEADS - 1))])
                pair_out(HEADS - 1, PAIRS - 1, 0)
                pair_out(HEADS - 1, PAIRS - 1, 1)
                pe.wait_ge(pj_done, pjd.value())
                if more:
                    pe.wait_ge(m_ready, mrd.value(1))
                for j in (DEN, RB, NUM, PROJ):
                    finish(j, HEADS - 1, LAST)

            pe.wait_ge(xb_ready, xb.next())
            for g in range(ET // 4):
                entry(("v", g), 0, 0, None)
            for c in range(CPB):
                for n in range(2):
                    entry(("prep", n), 0, 0, (0, c))
            pe.wait_ge(split_done, spl.value())
            for n in range(ABLK):
                entry(("max", n), 0, 0, None)
            max_rows()
            batches(pe, batch, [(xb, 1), (vr, 1), (rfr, RING), (spl, 4 * CHUNKS), (mc, CHUNKS), (mrd, CHUNKS), (exf, PAIRS * CHUNKS), (exd, PAIRS * CHUNKS),
                                (ocf, CHUNKS), (oc, CHUNKS), (dsd, 2 * CHUNKS), (rbc, CHUNKS), (aod, CHUNKS), (pjd, CPB)])


PAD = H + 2
ROWS = CH // W
TAPS = 9


def binary_conv(nc, d, X):
    with ExitStack() as ctx:
        sem = lambda n: ctx.enter_context(nc.semaphore(n))
        sb = lambda n, s, dt=F32: ctx.enter_context(nc.sbuf_tensor(n, s, dt))
        XS = sb("x_sign", [128, B, PAD, PAD], BF16)
        Y = sb("conv_sums", [128, N], F16)
        NEG = sb("neg_part", [128, 2, HW])
        wt, wr = sb("conv_wt", [128, TAPS * 128]), sb("conv_wr", [128, TAPS * 128])
        ws = sb("conv_wsign", [128, TAPS, 128], BF16)
        vec = sb("l1_vec", [128, 6])
        v = sb("l1_tmp", [128, 12])
        stats = sb("bn_stats", [128, B * CPB, 6])
        S = ctx.enter_context(nc.psum_tensor("conv_ps", [128, CPB, CH], F32))
        l1_in, edges, signed, wsigned = sem("l1_in"), sem("edges"), sem("signed"), sem("wsigned")
        cv_mm, cv_out, cv_stat, dve_step, act_step, relu_done, l1_done = (sem(n) for n in
            ("cv_mm", "cv_out", "cv_stat", "l1_dve", "l1_act", "relu_done", "l1_done"))
        block = ctx.enter_context(nc.Block())

        @block.sync
        def _(sp):
            sp.dma_start(vec[:], d["l1_vec"]).then_inc(l1_in, 16)
            sp.dma_start(wt[:], d["l1_wt"]).then_inc(l1_in, 16)
            sp.dma_start(wr[:], d["l1_wr"]).then_inc(l1_in, 16)

        @block.gpsimd
        def _(pool):
            for k, edge in enumerate((XS[:, :, 0, :], XS[:, :, PAD - 1, :], XS[:, :, 1:PAD - 1, 0:1], XS[:, :, 1:PAD - 1, PAD - 1:PAD])):
                nc.gpsimd.memset(edge, 0.0).then_inc(edges, 1)
                pool.wait_ge(edges, k + 1)

        @block.tensor
        def _(pe):
            pe.wait_ge(edges, 4)
            pe.wait_ge(wsigned, 1)
            for b in range(B):
                pe.wait_ge(signed, b + 1)
                for k in range(CPB):
                    if b > 0:
                        pe.wait_ge(cv_out, (b - 1) * CPB + k + 1)
                    for tap in range(TAPS):
                        dy, dx = tap // 3, tap % 3
                        m = nc.tensor.matmul(S[:, k, :], ws[:, tap, :], XS[:, b, k * ROWS + dy:k * ROWS + dy + ROWS, dx:dx + W],
                                             start=(tap == 0), stop=(tap == TAPS - 1))
                    m.then_inc(cv_mm, 1)

        @block.scalar
        def _(act):
            act.wait_ge(l1_in, 48)
            nc.scalar.activation(ws[:].rearrange("p a b -> p (a b)"), wt[:], ACT.Sign).then_inc(wsigned, 1)
            for b in range(B):
                nc.scalar.activation(XS[:, b, 1:H + 1, 1:W + 1], X[:, b * HW:(b + 1) * HW].rearrange("p (h w) -> p h w", h=H),
                                     ACT.Sign, bias=vec[:, 0:1]).then_inc(signed, 1)
            for k in range(B * CPB):
                act.wait_ge(cv_mm, k + 1)
                nc.scalar.copy(Y[:, k * CH:(k + 1) * CH], S[:, k % CPB, :]).then_inc(cv_out, 1)
            act.wait_ge(dve_step, V_VARY)
            nc.scalar.activation(v[:, 4:5], v[:, 3:4], ACT.Sqrt).then_inc(act_step, 1)
            for b in range(B):
                act.wait_ge(relu_done, 2 * b + 2)
                xb = X[:, b * HW:(b + 1) * HW]
                nc.scalar.activation(xb, xb, ACT.Identity, bias=v[:, 9:10]).then_inc(act_step, 1)

        @block.vector
        def _(dve):
            ch = Chain(dve, dve_step)
            dve.wait_ge(l1_in, 48)
            ch.step(nc.vector.tensor_reduce(v[:, 0:1], wr[:], AX.X, ALU.add, apply_absolute_value=True))
            ch.step(nc.vector.tensor_scalar(v[:, 0:1], v[:, 0:1], 1.0 / (TAPS * C), None, ALU.mult))
            for k in range(B * CPB):
                dve.wait_ge(cv_out, k + 1)
                nc.vector.bn_stats(stats[:, k, :], Y[:, k * CH:(k + 1) * CH]).then_inc(cv_stat, 1)
            dve.wait_ge(cv_stat, B * CPB)
            ch.step(nc.vector.bn_aggr(v[:, 1:3], stats[:].rearrange("p k s -> p (k s)")))
            ch.step(nc.vector.tensor_scalar(v[:, 3:4], v[:, 2:3], v[:, 0:1], v[:, 0:1], ALU.mult, ALU.mult))
            ch.step(nc.vector.tensor_scalar(v[:, 3:4], v[:, 3:4], 1e-5, None, ALU.add))
            assert ch.done.n == V_VARY
            dve.wait_ge(act_step, 1)
            ch.step(nc.vector.reciprocal(v[:, 5:6], v[:, 4:5]))
            ch.step(nc.vector.tensor_scalar(v[:, 6:7], v[:, 5:6], v[:, 0:1], vec[:, 1:2], ALU.mult, ALU.mult))
            ch.step(nc.vector.tensor_scalar(v[:, 7:8], v[:, 6:7], v[:, 1:2], -1.0, ALU.mult, ALU.mult))
            ch.step(nc.vector.tensor_scalar(v[:, 8:9], v[:, 7:8], vec[:, 2:3], vec[:, 3:4], ALU.add, ALU.add))
            ch.step(nc.vector.tensor_scalar(v[:, 9:10], v[:, 8:9], vec[:, 5:6], None, ALU.add))
            ch.step(nc.vector.tensor_scalar(v[:, 10:11], vec[:, 4:5], -1.0, None, ALU.add))
            for b in range(B + 1):
                if b < B:
                    xb = X[:, b * HW:(b + 1) * HW]
                    nc.vector.scalar_tensor_tensor(xb, Y[:, b * HW:(b + 1) * HW], v[:, 6:7], xb, ALU.mult, ALU.add).then_inc(relu_done, 1)
                    dve.wait_ge(relu_done, 2 * b + 1)
                    if b >= 2:
                        dve.wait_ge(l1_done, b - 1)
                    nc.vector.tensor_scalar(NEG[:, b % 2, :], xb, v[:, 8:9], 0.0, ALU.add, ALU.min).then_inc(relu_done, 1)
                if b >= 1:
                    xb = X[:, (b - 1) * HW:b * HW]
                    dve.wait_ge(relu_done, 2 * b)
                    dve.wait_ge(act_step, 1 + b)
                    nc.vector.scalar_tensor_tensor(xb, NEG[:, (b - 1) % 2, :], v[:, 10:11], xb, ALU.mult, ALU.add).then_inc(l1_done, 1)


V_VARY = 5


WS = 8
NW = W // WS
WT = WS * WS
DI = 256
DH = DI // 128
NS = 16
SG = 2
GR = NS // SG
DTR = 8
KC = 4
NCH = B * CPB
BCR = 3 * 2 * NS
PAIRED = (0, 2, 3, 6)


def mamba(nc, d, X):
    with ExitStack() as ctx:
        sem = lambda n: ctx.enter_context(nc.semaphore("l2_" + n))
        sb = lambda n, s, dt=F32: ctx.enter_context(nc.sbuf_tensor("l2_" + n, s, dt))
        w_in, w_dt, w_out = sb("w_in", [128, 2 * DI]), sb("w_dt", [BCR + DTR, DI]), sb("w_out", [128, DH, C])
        w_bcr, onehot = sb("w_bcr", [128, DH, BCR + DTR]), sb("onehot", [BCR, 2 * NS, 128], BF16)
        taps = sb("taps", [128, DH, KC, 128])
        conv_bias = sb("conv_bias", [128, DH, KC])
        ident, avg, ones = sb("ident", [128, 128]), sb("avg", [128, 128]), sb("ones", [128, 128])
        Am = sb("A", [128, DH * NS])
        vec = sb("vec", [128, 22])
        with ExitStack() as c1:
            sb1 = lambda n, s, dt=F32: c1.enter_context(nc.sbuf_tensor("l2_" + n, s, dt))
            oh32 = sb1("oh32", [BCR, 2 * NS])
            ps = c1.enter_context(nc.psum_tensor("l2_setup_ps", [128, DH + 1, 512], F32))
            w_loaded, s_pe, s_act, s_dve = sem("w_loaded"), sem("s_pe"), sem("s_act"), sem("s_dve")
            block = c1.enter_context(nc.Block())
            loads = [(w_in, "l2_w_in"), (w_out, "l2_w_out"), (w_bcr, "l2_w_bcr"), (w_dt, "l2_w_dt"), (ident, "ident"), (Am, "l2_alog"),
                     (vec, "l2_vec"), (oh32, "l2_onehot")]

            @block.sync
            def _(sp):
                for dst, name in loads:
                    sp.dma_start(dst[:], d[name]).then_inc(w_loaded, 16)

            @block.tensor
            def _(pe):
                pe.wait_ge(w_loaded, 16 * len(loads))
                for k in range(4):
                    nc.tensor.matmul(ps[:, DH, k:k + 1], w_in[:, k * 128:(k + 1) * 128], vec[:, 13:14], start=True, stop=True)
                pe.wait_ge(s_dve, 3 + DH * KC)
                for h in range(DH):
                    m = nc.tensor.matmul(ps[:, h, :], ones[:], taps[:, h].rearrange("p k c -> p (k c)"), start=True, stop=True)
                m.then_inc(s_pe, 1)

            @block.scalar
            def _(act):
                act.wait_ge(w_loaded, 16 * len(loads))
                nc.scalar.activation(Am[:], Am[:], ACT.Exp).then_inc(s_act, 1)

            @block.vector
            def _(dve):
                ch = Chain(dve, s_dve)
                dve.wait_ge(w_loaded, 16 * len(loads))
                ch.step(nc.vector.memset(avg[:], 1.0 / C))
                ch.step(nc.vector.memset(ones[:], 1.0))
                ch.step(nc.vector.tensor_copy(onehot[:], oh32[:].unsqueeze(2).to_broadcast([BCR, 2 * NS, 128])))
                for h in range(DH):
                    for k in range(KC):
                        ch.step(nc.vector.tensor_scalar(taps[:, h, k, :], ident[:], vec[:, 14 + h * KC + k:15 + h * KC + k], None, ALU.mult))
                dve.wait_ge(s_pe, 1)
                ch.step(nc.vector.tensor_tensor(vec[:, 8:12], vec[:, 8:12], ps[:, DH, 0:4], ALU.add))
                ch.step(nc.vector.tensor_scalar(w_in[:], w_in[:], vec[:, 12:13], None, ALU.mult))
                for h in range(DH):
                    ch.step(nc.vector.tensor_tensor(taps[:, h], w_in[:, h * 128:(h + 1) * 128].unsqueeze(1).to_broadcast([128, KC, 128]),
                                                    ps[:, h, :].rearrange("p (k c) -> p k c", k=KC), ALU.mult))
                    for t in range(KC):
                        before = vec[:, 2 + h:3 + h] if t == 0 else conv_bias[:, h, t - 1:t]
                        w = 14 + h * KC + KC - 1 - t
                        ch.step(nc.vector.scalar_tensor_tensor(conv_bias[:, h, t:t + 1], vec[:, w:w + 1], vec[:, 8 + h:9 + h], before, ALU.mult, ALU.add))
                dve.wait_ge(s_act, 1)
                ch.step(nc.vector.tensor_scalar(Am[:], Am[:], -1.0, None, ALU.mult))

        XCEN, XSQ, DIAG = sb("x_cen", [128, CH]), sb("x_sq", [128, CH]), sb("rstd_diag", [128, 4, 128])
        std = sb("std", [128, 4])
        TN = sb("x_norm", [128, NW, KC - 1 + WT])
        XC, ZS = sb("xc", [128, 2, DH, CH]), sb("z_silu", [128, 2, DH, CH])
        DEL, DTX = sb("delta", [128, 2, DH, CH]), sb("delta_x", [128, 2, DH, CH])
        EX, UU = sb("exp_abs", [128, DH, CH]), sb("one_plus", [128, DH, CH])
        BCD = sb("bc_rank", [BCR + DTR, CH])
        BCS, R1, MID = sb("bc_split", [BCR, 2, CH], BF16), sb("bc_rest", [BCR, CH]), sb("bc_mid", [BCR, CH], BF16)
        DA, HB, HC = sb("decay", [128, 2, DH, SG, CH]), sb("state", [128, 2, DH, SG, CH]), sb("state_c", [128, 2, DH, SG, CH])
        CB = sb("c_rows", [128, 2, SG, CH])
        YG, OT = sb("y_gated", [128, DH, CH]), sb("out_rows", [128, CH])
        pst = lambda n, s: ctx.enter_context(nc.psum_tensor("l2_" + n, s, F32))
        PB, PC, PY, PF = pst("b_rows", [128, SG, CH]), pst("c_rows_ps", [128, SG, CH]), pst("y_acc", [128, DH, CH]), pst("front", [128, 2, CH])

        zeroed = sem("zeroed")
        mu_mm, centred, squared, var_mm, std_done, diag, rs_mm, normed = (sem(n) for n in
            ("mu_mm", "centred", "squared", "var_mm", "std_done", "diag", "rs_mm", "normed"))
        var_ln, cv_mm, xc_done, z_mm, zs_done, bc_mm, bc_copied, split, dp_mm = (sem(n) for n in
            ("var_ln", "cv_mm", "xc_done", "z_mm", "zs_done", "bc_mm", "bc_copied", "split", "dp_mm"))
        abs_done, relu_done, exp_done, plus_done, ln_done, delta, dtx_done = (sem(n) for n in
            ("abs_done", "relu_done", "exp_done", "plus_done", "ln_done", "delta", "dtx_done"))
        bb_mm, cb_mm, cb_done, da_done, b_done, scanned, hc_done, paired, acc_mm = (sem(n) for n in
            ("bb_mm", "cb_mm", "cb_done", "da_done", "b_done", "scanned", "hc_done", "paired", "acc_mm"))
        gated, op_mm, ot_done, added = sem("gated"), sem("op_mm"), sem("ot_done"), sem("added")
        block = ctx.enter_context(nc.Block())

        def chunks(eng, step, per_chunk):
            step(0, 0, False, True)
            with counted_loop(eng, (NCH - 2) // 2, *[(t, 2 * k) for t, k in per_chunk]) as turn:
                step(turn * 2 + 1, 1, True, True)
                step(turn * 2 + 2, 0, True, True)
            step(NCH - 1, 1, True, False)

        cols = lambda n: bass.ds(n * CH, CH)
        windows = lambda ap: ap.rearrange("p (h n w) -> p h n w", h=WS, n=NW)
        by_window = lambda ap: ap.rearrange("p (n h w) -> p h n w", n=NW, h=WS)

        @block.tensor
        def _(pe):
            relu, sq, dg, nrm, xc, zs, bcc, spl = Tally(1), Tally(), Tally(), Tally(), Tally(), Tally(), Tally(), Tally()
            bfree, cfree, hcd, prd, gt, ad = Tally(0), Tally(0), Tally(2), Tally(), Tally(), Tally()
            pe.wait_ge(zeroed, 6)
            tokens = TN[:, :, KC - 1:]

            def convolve(h):
                for k in range(KC):
                    m = nc.tensor.matmul(PF[:, h, :], taps[:, h, k, :], TN[:, :, k:k + WT], start=(k == 0), stop=(k == KC - 1))
                m.then_inc(cv_mm, 1)

            def front(n, q, g, back_q=None):
                if g == 0:
                    pe.wait_ge(relu_done, relu.value())
                    relu.n += DH
                    nc.tensor.matmul(PF[:, 1, :], avg[:], X[:, cols(n)], start=True, stop=True).then_inc(mu_mm, 1)
                if g == 1:
                    pe.wait_ge(squared, sq.next())
                    for k in range(4):
                        m = nc.tensor.matmul(PF[:, 1, k:k + 1], XSQ[:, k * 128:(k + 1) * 128], avg[:, 0:1], start=True, stop=True)
                    m.then_inc(var_mm, 1)
                if g == 2:
                    pe.wait_ge(diag, dg.next())
                    nc.tensor.matmul(PF[:, 1, :], ones[:], DIAG[:].rearrange("p k c -> p (k c)"), start=True, stop=True).then_inc(rs_mm, 1)
                if g == 3:
                    pe.wait_ge(normed, nrm.next())
                    convolve(0)
                if g == 4:
                    convolve(1)
                    if back_q is not None:
                        b_rows(6, back_q)
                    for h in range(DH):
                        pe.wait_ge(xc_done, xc.next())
                        nc.tensor.matmul(PF[:, h, :], w_in[:, DI + h * 128:DI + (h + 1) * 128], tokens, start=True, stop=True).then_inc(z_mm, 1)
                if g == 5:
                    pe.wait_ge(zs_done, zs.next())
                    for h in range(DH):
                        m = nc.tensor.matmul(PF[0:BCR + DTR, 0, :], w_bcr[:, h, :], XC[:, q, h, :], start=(h == 0), stop=(h == DH - 1))
                    m.then_inc(bc_mm, 1)
                if g == 6:
                    pe.wait_ge(zs_done, zs.next())
                    pe.wait_ge(bc_copied, bcc.next())
                    for o in range(DH):
                        nc.tensor.matmul(PF[:, 1 - o, :], w_dt[:, o * 128:(o + 1) * 128], BCD[:], start=True, stop=True).then_inc(dp_mm, 1)

            def b_rows(g, q):
                pe.wait_ge(b_done, bfree.next())
                for k in range(SG):
                    m = nc.tensor.matmul(PB[:, k, :], onehot[:, g * SG + k, :], BCS[:, q, :], start=True, stop=True)
                m.then_inc(bb_mm, 1)

            def c_rows(g, q):
                pe.wait_ge(cb_done, cfree.next())
                for k in range(SG):
                    m = nc.tensor.matmul(PC[:, k, :], onehot[:, NS + g * SG + k, :], BCS[:, q, :], start=True, stop=True)
                m.then_inc(cb_mm, 1)

            def accumulate(k):
                hcd.n += 1
                if k in PAIRED:
                    pe.wait_ge(paired, prd.next())
                else:
                    pe.wait_ge(hc_done, hcd.value())
                if k == 0 and not state["first"]:
                    pe.wait_ge(gated, gt.value())
                states = range(1 if k in PAIRED else SG)
                for h in range(DH):
                    for i in states:
                        m = nc.tensor.matmul(PY[:, h, :], ident[:], HC[:, k % 2, h, i, :], start=(k == 0 and i == 0), stop=(k == GR - 1 and i == states[-1]))
                m.then_inc(acc_mm, 1)

            state = {"first": True}

            def project_out():
                gt.n += 3
                pe.wait_ge(gated, gt.value())
                for h in range(DH):
                    m = nc.tensor.matmul(PF[:, 0, :], w_out[:, h, :], YG[:, h, :], start=(h == 0), stop=(h == DH - 1))
                m.then_inc(op_mm, 1)

            def chunk(i, q, back, more):
                for g in range(GR):
                    if g == 2 and back:
                        project_out()
                    if g >= 2:
                        accumulate(g - 2)
                    elif back:
                        accumulate(GR - 2 + g)
                    if g < GR - 1:
                        if g != 5 or not more:
                            b_rows(g + 1, q)
                        c_rows(g + 1, q)
                    elif more:
                        spl.n += 5
                        pe.wait_ge(split, spl.value())
                        b_rows(0, 1 - q)
                        c_rows(0, 1 - q)
                    if more:
                        if g == 3 and back:
                            pe.wait_ge(ot_done, ad.next())
                        front(i + 1, 1 - q, g, q)
                state["first"] = False
                if not more:
                    ad.n += 1

            for g in range(GR - 1):
                front(0, 0, g)
            spl.n += 5
            pe.wait_ge(split, spl.value())
            b_rows(0, 0)
            c_rows(0, 0)
            chunks(pe, chunk, [(relu, DH), (sq, 1), (dg, 1), (nrm, 1), (xc, DH), (zs, 2), (bcc, 1), (spl, 5),
                               (bfree, GR), (cfree, GR), (hcd, GR), (prd, len(PAIRED)), (gt, 3), (ad, 1)])
            accumulate(GR - 2)
            accumulate(GR - 1)
            project_out()

        @block.scalar
        def _(act):
            cen, var, vln, cvm, zm, bcm, dpm, pls, dlt = (Tally() for _ in range(9))
            cbm, hcf, scf, opm, ab, ln = Tally(), Tally(0), Tally(0), Tally(), Tally(), Tally()
            act.wait_ge(zeroed, 6)
            nc.scalar.preload_act_table_set("natural_log_exp_and_others")

            def front(n, q, g):
                if g == 0:
                    act.wait_ge(centred, cen.next())
                    nc.scalar.activation(XSQ[:], XCEN[:], ACT.Square).then_inc(squared, 1)
                if g == 1:
                    act.wait_ge(var_mm, var.next())
                    nc.scalar.activation(std[:], PF[:, 1, 0:4], ACT.Ln, bias=vec[:, 0:1]).then_inc(var_ln, 1)
                    act.wait_ge(var_ln, vln.next())
                    nc.scalar.activation(std[:], std[:], ACT.Exp, scale=-0.5).then_inc(std_done, 1)
                if g == 4:
                    for h in range(DH):
                        act.wait_ge(cv_mm, cvm.next())
                        src, dst = (ap.rearrange("p (n t) -> p n t", n=NW) for ap in (PF[:, h, :], XC[:, q, h, :]))
                        for t in range(KC):
                            ts = slice(t, t + 1) if t < KC - 1 else slice(t, WT)
                            e = nc.scalar.activation(dst[:, :, ts], src[:, :, ts], ACT.Silu, bias=conv_bias[:, h, t:t + 1])
                        e.then_inc(xc_done, 1)
                    for h in range(DH):
                        act.wait_ge(z_mm, zm.next())
                        nc.scalar.activation(ZS[:, q, h, :], PF[:, h, :], ACT.Silu, bias=vec[:, 10 + h:11 + h]).then_inc(zs_done, 1)
                    nc.scalar.preload_act_table_set("natural_log_exp_and_others")
                if g == 5:
                    act.wait_ge(bc_mm, bcm.next())
                    nc.scalar.copy(BCD[:], PF[0:BCR + DTR, 0, :]).then_inc(bc_copied, 1)
                if g == 6:
                    for o in range(DH):
                        act.wait_ge(dp_mm, dpm.next())
                        nc.scalar.activation(EX[:, o, :], PF[:, 1 - o, :], ACT.Abs, bias=vec[:, 4 + o:5 + o]).then_inc(abs_done, 1)
                    ab.n += DH
                    act.wait_ge(abs_done, ab.value())
                    nc.scalar.activation(EX[:], EX[:], ACT.Exp, scale=-1.0).then_inc(exp_done, 1)
                if g == 7:
                    nc.scalar.preload_act_table_set("natural_log")
                    act.wait_ge(plus_done, pls.next())
                    nc.scalar.activation(DEL[:, q], UU[:], ACT.Ln).then_inc(ln_done, 1)
                    nc.scalar.preload_act_table_set("natural_log_exp_and_others")

            def decays(q, g):
                act.wait_ge(scanned, scf.next())
                for h in range(DH):
                    for k in range(SG):
                        e = nc.scalar.activation(DA[:, g % 2, h, k, :].rearrange("p (n t) -> p n t", n=NW)[:, :, 1:],
                                                 DEL[:, q, h, :].rearrange("p (n t) -> p n t", n=NW)[:, :, 1:], ACT.Exp,
                                                 scale=Am[:, h * NS + g * SG + k:h * NS + g * SG + k + 1])
                e.then_inc(da_done, 1)

            def chunk(i, q, back, more):
                dlt.n += 3
                act.wait_ge(delta, dlt.value())
                decays(q, 0)
                for g in range(GR):
                    act.wait_ge(cb_mm, cbm.next())
                    act.wait_ge(hc_done, hcf.next())
                    nc.scalar.copy(CB[:, g % 2], PC[:]).then_inc(cb_done, 1)
                    if more and g == 5:
                        front(i + 1, 1 - q, 4)
                    if g < GR - 1:
                        decays(q, g + 1)
                    if g == 2 and back:
                        act.wait_ge(op_mm, opm.next())
                        nc.scalar.activation(windows(OT[:]), by_window(PF[:, 0, :]), ACT.Identity, bias=vec[:, 1:2]).then_inc(ot_done, 1)
                    if more and g < GR - 1 and g != 4:
                        front(i + 1, 1 - q, g)
                    if more and g == GR - 2:
                        front(i + 1, 1 - q, g + 1)

            for g in range(GR):
                front(0, 0, g)
            chunks(act, chunk, [(cen, 1), (var, 1), (vln, 1), (cvm, DH), (zm, DH), (bcm, 1), (dpm, DH), (pls, 1), (dlt, 3),
                                (cbm, GR), (hcf, GR), (scf, GR), (opm, 1), (ab, DH)])
            act.wait_ge(op_mm, opm.next())
            nc.scalar.activation(windows(OT[:]), by_window(PF[:, 0, :]), ACT.Identity, bias=vec[:, 1:2]).then_inc(ot_done, 1)

        @block.vector
        def _(dve):
            zero = [TN[:, :, 0:KC - 1]] + [DA[:, s, h].rearrange("p k (n t) -> p (k n) t", n=NW)[:, :, 0:1] for s in range(2) for h in range(DH)]
            for z in zero:
                nc.vector.memset(z, 0.0).then_inc(zeroed, 1)
            nc.vector.memset(vec[:, 0:1], 1e-5).then_inc(zeroed, 1)
            for n, (s, k) in enumerate(((relu_done, 1), (b_done, 1), (cb_done, 1), (scanned, 2), (hc_done, 2), (acc_mm, 2))):
                nc.vector.memset(std[:, 0:1], 0.0).then_inc(s, k)
                dve.wait_ge(s, k)
            mum, std_, rsm, bcm, spl, abs_, ex, ln, dl = (Tally() for _ in range(9))
            bbm, hcf, bd, da, scn, accd, gt, otd, rlt = Tally(), Tally(0), Tally(1), Tally(), Tally(2), Tally(2), Tally(), Tally(), Tally(1)
            addn = Tally()

            def front(n, q, g):
                if g == 0:
                    dve.wait_ge(mu_mm, mum.next())
                    nc.vector.tensor_tensor(XCEN[:], X[:, cols(n)], PF[:, 1, :], ALU.subtract).then_inc(centred, 1)
                if g == 1:
                    dve.wait_ge(std_done, std_.next())
                    nc.vector.tensor_tensor(DIAG[:], ident[:].unsqueeze(1).to_broadcast([128, 4, 128]), std[:].unsqueeze(2).to_broadcast([128, 4, 128]),
                                            ALU.mult).then_inc(diag, 1)
                if g == 2:
                    dve.wait_ge(rs_mm, rsm.next())
                    nc.vector.tensor_tensor(TN[:, :, KC - 1:].rearrange("p n (h w) -> p h n w", h=WS), windows(XCEN[:]), windows(PF[:, 1, :]), ALU.mult).then_inc(normed, 1)
                if g == 5:
                    dve.wait_ge(bc_copied, bcm.next())
                    nc.vector.tensor_copy(BCS[:, q, :], BCD[0:BCR, :]).then_inc(split, 1)
                    dve.wait_ge(split, spl.next())
                    nc.vector.tensor_tensor(R1[:], BCD[0:BCR, :], BCS[:, q, :], ALU.subtract).then_inc(split, 1)
                    dve.wait_ge(split, spl.next())
                    nc.vector.tensor_copy(BCS[32:64, q, :], R1[32:64, :]).then_inc(split, 1)
                    nc.vector.tensor_copy(MID[64:96, :], R1[64:96, :]).then_inc(split, 1)
                    spl.n += 2
                    dve.wait_ge(split, spl.value())
                    nc.vector.tensor_tensor(BCS[64:96, q, :], R1[64:96, :], MID[64:96, :], ALU.subtract).then_inc(split, 1)
                    spl.n += 1
                if g == 6:
                    for o in range(DH):
                        dve.wait_ge(abs_done, abs_.next())
                        nc.vector.tensor_scalar(DTX[:, q, o, :], PF[:, 1 - o, :], vec[:, 4 + o:5 + o], 0.0, ALU.add, ALU.max).then_inc(relu_done, 1)
                        rlt.n += 1
                if g == 6:
                    dve.wait_ge(exp_done, ex.next())
                    nc.vector.tensor_scalar(UU[:], EX[:], 1.0, None, ALU.add).then_inc(plus_done, 1)
                if g == 7:
                    dve.wait_ge(ln_done, ln.next())
                    nc.vector.scalar_tensor_tensor(UU[:], UU[:], -1.0, EX[:], ALU.add, ALU.subtract).then_inc(delta, 1)
                    dve.wait_ge(delta, dl.next())
                    nc.vector.tensor_tensor(DEL[:, q], DEL[:, q], UU[:], ALU.subtract).then_inc(delta, 1)
                    dve.wait_ge(delta, dl.next())
                    dve.wait_ge(relu_done, rlt.value())
                    nc.vector.tensor_tensor(DEL[:, q], DEL[:, q], DTX[:, q], ALU.add).then_inc(delta, 1)
                    dve.wait_ge(delta, dl.next())
                    nc.vector.tensor_tensor(DTX[:, q], DEL[:, q], XC[:, q], ALU.mult).then_inc(dtx_done, 1)

            def gate(q):
                accd.n += GR
                dve.wait_ge(acc_mm, accd.value())
                for h in range(DH):
                    nc.vector.scalar_tensor_tensor(YG[:, h, :], XC[:, q, h, :], vec[:, 6 + h:7 + h], PY[:, h, :], ALU.mult, ALU.add).then_inc(gated, 1)
                gt.n += 2
                dve.wait_ge(gated, gt.value())
                nc.vector.tensor_tensor(YG[:], YG[:], ZS[:, q], ALU.mult).then_inc(gated, 1)
                gt.n += 1

            def residual(n):
                dve.wait_ge(ot_done, otd.next())
                nc.vector.tensor_tensor(X[:, cols(n)], X[:, cols(n)], OT[:], ALU.add).then_inc(added, 1)
                addn.n += 1

            def chunk(i, q, back, more):
                dtxd.n += 1
                dve.wait_ge(dtx_done, dtxd.value())
                for g in range(GR):
                    dve.wait_ge(bb_mm, bbm.next())
                    dve.wait_ge(hc_done, hcf.next())
                    nc.vector.tensor_tensor(HB[:, g % 2], PB[:].unsqueeze(1).to_broadcast([128, DH, SG, CH]),
                                            DTX[:, q].unsqueeze(2).to_broadcast([128, DH, SG, CH]), ALU.mult).then_inc(b_done, 1)
                    if g == 3 and back:
                        residual(i - 1)
                    if more and 1 <= g < GR - 1:
                        front(i + 1, 1 - q, g - 1)
                    if g == GR - 1 and more:
                        front(i + 1, 1 - q, g)
                    dve.wait_ge(b_done, bd.next())
                    dve.wait_ge(da_done, da.next())
                    flat = lambda ap: ap.rearrange("p h k t -> p (h k t)")
                    nc.vector.tensor_tensor_scan(flat(HB[:, g % 2]), flat(DA[:, g % 2]), flat(HB[:, g % 2]), 0.0, ALU.mult, ALU.add).then_inc(scanned, 1)
                    if g == 1 and back:
                        gate(1 - q)
                    if more and g == GR - 2:
                        front(i + 1, 1 - q, g)

            dtxd = Tally()
            for g in range(GR):
                front(0, 0, g)
            chunks(dve, chunk, [(mum, 1), (std_, 1), (rsm, 1), (bcm, 1), (spl, 5), (abs_, DH), (rlt, DH), (ex, 1), (ln, 1), (dl, 3),
                                (bbm, GR), (hcf, GR), (bd, GR), (da, GR), (accd, GR), (gt, 3), (otd, 1), (addn, 1), (dtxd, 1)])
            gate(1)
            residual(NCH - 1)

        @block.gpsimd
        def _(pool):
            scn, cbd, accf, hcd = Tally(2), Tally(1), Tally(0), Tally(2)
            pool.wait_ge(zeroed, 6)

            def chunk(i, q, back, more):
                for g in range(GR):
                    pool.wait_ge(scanned, scn.next())
                    pool.wait_ge(cb_done, cbd.next())
                    pool.wait_ge(acc_mm, accf.next())
                    nc.gpsimd.tensor_tensor(HC[:, g % 2], HB[:, g % 2], CB[:, g % 2].unsqueeze(1).to_broadcast([128, DH, SG, CH]), ALU.mult).then_inc(hc_done, 1)
                    hcd.n += 1
                    if g in PAIRED:
                        pool.wait_ge(hc_done, hcd.value())
                        nc.gpsimd.tensor_tensor(HC[:, g % 2, :, 0, :], HC[:, g % 2, :, 0, :], HC[:, g % 2, :, 1, :], ALU.add).then_inc(paired, 1)

            chunks(pool, chunk, [(scn, GR), (cbd, GR), (accf, GR), (hcd, GR)])


H3 = 8
HC3 = C // H3
TILES = CH // 128


def linear_attention(nc, d, X, out):
    with ExitStack() as ctx:
        sem = lambda n: ctx.enter_context(nc.semaphore(n))
        sb = lambda n, s, dt=F32: ctx.enter_context(nc.sbuf_tensor(n, s, dt))
        kvw, qw, o1, o2, mask, ident = sb("kv_w", [128, 256]), sb("q_w3", [128, 128]), sb("o1_w", [128, 128]), sb("o2_w", [128, 128]), sb("kv_mask", [128, 128]), sb("ident3", [128, 128])
        lnw, lnb = sb("ln3_w", [128, 256]), sb("ln3_b", [128, 256])
        G = sb("o1_map", [128, B, 128])
        l3_in = sem("l3_in")
        with ExitStack() as c1:
            sb1 = lambda n, s, dt=F32: c1.enter_context(nc.sbuf_tensor(n, s, dt))
            XB = sb1("x_batch3", [128, HW])
            SQ, KV = sb1("kv_sq", [128, 2, TILES * 256]), sb1("kv_norm", [128, 3, TILES * 256])
            st = sb1("kv_std", [128, 2, TILES * 16])
            wm = sb1("w_mean", [128, 16])
            kvm, ai = sb1("kv_masked", [128, 128]), sb1("att_map", [128, 128])
            PS = c1.enter_context(nc.psum_tensor("kv_ps", [128, 2, TILES * 256], F32))
            ACC = c1.enter_context(nc.psum_tensor("kv_acc", [128, 512], F32))
            MAP = c1.enter_context(nc.psum_tensor("map_ps", [128, 512], F32))
            xb_ready, kv_mm, sq_done, ss_done, std_done, std_step, scaled, shifted, acc_mm, kvm_done, ai_mm, ai_done, g_mm, g_done, w_step = (
                sem("l3_" + n) for n in ("xb_ready", "kv_mm", "sq_done", "ss_done", "std_done", "std_step", "scaled", "shifted", "acc_mm",
                                         "kvm_done", "ai_mm", "ai_done", "g_mm", "g_done", "w_step"))
            norm_done = sem("l3_norm_done")
            block = c1.enter_context(nc.Block())

            @block.sync
            def _(sp):
                for dst, name in ((kvw, "l3_kvw"), (qw, "l3_qw"), (o1, "l3_o1"), (o2, "l3_o2"), (mask, "l3_mask"), (ident, "ident"),
                                  (lnw, "l3_lnw"), (lnb, "l3_lnb")):
                    sp.dma_start(dst[:], d[name]).then_inc(l3_in, 16)

            @block.tensor
            def _(pe):
                xb, sc, sh, gd, kd, ad = Tally(), Tally(), Tally(), Tally(), Tally(), Tally()
                pe.wait_ge(w_step, 3)

                def project(k):
                    if k >= 2:
                        pe.wait_ge(norm_done, sc.next())
                    for i in range(TILES):
                        e = k * TILES + i
                        m = nc.tensor.matmul(PS[:, k % 2, i * 256:(i + 1) * 256], XB[:, e * 128:(e + 1) * 128], kvw[:], start=True, stop=True)
                    m.then_inc(kv_mm, 1)

                def outer(k):
                    pe.wait_ge(shifted, sh.next())
                    for i in range(TILES):
                        m = nc.tensor.matmul(ACC[:, 0:128], KV[:, k % 3, i * 256:i * 256 + 128], KV[:, k % 3, i * 256 + 128:(i + 1) * 256],
                                             start=(k == 0 and i == 0), stop=(k == CPB - 1 and i == TILES - 1))
                    m.then_inc(acc_mm, 1)

                with counted_loop(pe, B, (xb, 1), (sc, CPB), (sh, CPB), (kd, 1), (ad, 1)) as b:
                    pe.wait_ge(xb_ready, xb.next())
                    for k in range(CPB):
                        project(k)
                        if k >= 1:
                            outer(k - 1)
                    outer(CPB - 1)
                    sc.n += 2
                    pe.wait_ge(kvm_done, kd.next())
                    nc.tensor.matmul(MAP[:, 0:128], kvm[:], qw[:], start=True, stop=True).then_inc(ai_mm, 1)
                    pe.wait_ge(ai_done, ad.next())
                    nc.tensor.matmul(MAP[:, 128:256], ai[:], o1[:], start=True, stop=True).then_inc(g_mm, 1)

            @block.scalar
            def _(act):
                mm, ss, st_ = Tally(), Tally(), Tally()
                sqf = Tally()
                act.wait_ge(l3_in, 16 * 8)

                with counted_loop(act, B, (mm, CPB), (ss, CPB), (sqf, CPB)) as b:
                    for k in range(CPB):
                        act.wait_ge(kv_mm, mm.next())
                        act.wait_ge(ss_done, sqf.next(0))
                        nc.scalar.activation(SQ[:, k % 2, :], PS[:, k % 2, :], ACT.Square).then_inc(sq_done, 1)
                        act.wait_ge(ss_done, ss.next(2))
                        nc.scalar.activation(st[:, k % 2, :], st[:, k % 2, :], ACT.Sqrt, scale=1.0 / (HC3 - 1)).then_inc(std_done, 1)

            @block.vector
            def _(dve):
                dve.wait_ge(l3_in, 16 * 8)
                g3 = kvw[:].rearrange("p (g c) -> p g c", c=HC3)
                nc.vector.tensor_reduce(wm[:], g3, AX.X, ALU.add).then_inc(w_step, 1)
                dve.wait_ge(w_step, 1)
                nc.vector.tensor_scalar(wm[:], wm[:], 1.0 / HC3, None, ALU.mult).then_inc(w_step, 1)
                dve.wait_ge(w_step, 2)
                nc.vector.tensor_tensor(g3, g3, wm[:].unsqueeze(2).to_broadcast([128, 16, HC3]), ALU.subtract).then_inc(w_step, 1)
                for s, k in ((ss_done, 2), (acc_mm, 3)):
                    nc.vector.memset(st[:, 0, 0:1], 0.0).then_inc(s, k)
                    dve.wait_ge(s, k)
                sq, sd, stp, nd, am, amm, gm, aim, gmm = (Tally() for _ in range(9))
                accf = Tally()
                with counted_loop(dve, B, (sq, CPB), (sd, CPB), (stp, 2 * CPB), (nd, CPB), (accf, CPB), (am, CPB), (aim, 1), (gmm, 1)) as b:
                    nc.vector.tensor_copy(XB[:], X[:, bass.ds(b * HW, HW)]).then_inc(xb_ready, 1)
                    for k in range(CPB):
                        dve.wait_ge(sq_done, sq.next())
                        nc.vector.tensor_reduce(st[:, k % 2, :], SQ[:, k % 2, :].rearrange("p (g c) -> p g c", c=HC3), AX.X, ALU.add).then_inc(ss_done, 1)
                        dve.wait_ge(std_done, sd.next())
                        nc.vector.tensor_scalar(st[:, k % 2, :], st[:, k % 2, :], 1e-5, None, ALU.add).then_inc(std_step, 1)
                        dve.wait_ge(std_step, stp.next())
                        nc.vector.reciprocal(st[:, k % 2, :], st[:, k % 2, :]).then_inc(std_step, 1)
                        dve.wait_ge(std_step, stp.next())
                        dve.wait_ge(acc_mm, accf.next())
                        nc.vector.tensor_tensor(KV[:, k % 3, :].rearrange("p (g c) -> p g c", c=HC3), PS[:, k % 2, :].rearrange("p (g c) -> p g c", c=HC3),
                                                st[:, k % 2, :].unsqueeze(2).to_broadcast([128, TILES * 16, HC3]), ALU.mult).then_inc(norm_done, 1)
                        dve.wait_ge(norm_done, nd.next())
                        kv4 = KV[:, k % 3, :].rearrange("p (t c) -> p t c", t=TILES)
                        nc.vector.tensor_tensor(kv4, kv4, lnw[:].unsqueeze(1).to_broadcast([128, TILES, 256]), ALU.mult).then_inc(scaled, 1)
                    am.n += CPB
                    dve.wait_ge(acc_mm, am.value(3))
                    nc.vector.tensor_tensor(kvm[:], ACC[:, 0:128], mask[:], ALU.mult).then_inc(kvm_done, 1)
                    dve.wait_ge(ai_mm, aim.next())
                    nc.vector.tensor_tensor(ai[:], MAP[:, 0:128], ident[:], ALU.add).then_inc(ai_done, 1)
                    dve.wait_ge(g_mm, gmm.next())
                    nc.vector.tensor_copy(G[:, bass.ds(b, 1), :], MAP[:, 128:256].rearrange("p (a c) -> p a c", a=1)).then_inc(g_done, 1)

            @block.gpsimd
            def _(pool):
                sc = Tally()
                pool.wait_ge(l3_in, 16 * 8)
                with counted_loop(pool, B, (sc, CPB)) as b:
                    for k in range(CPB):
                        pool.wait_ge(scaled, sc.next())
                        kv4 = KV[:, k % 3, :].rearrange("p (t c) -> p t c", t=TILES)
                        nc.gpsimd.tensor_tensor(kv4, kv4, lnb[:].unsqueeze(1).to_broadcast([128, TILES, 256]), ALU.add).then_inc(shifted, 1)

        U, R, O = sb("gelu_in", [128, 2, CH]), sb("mlp_sum", [128, 2, CH]), sb("out_tile", [128, 4, CH])
        PU, PO = ctx.enter_context(nc.psum_tensor("u_ps", [128, 2, CH], F32)), ctx.enter_context(nc.psum_tensor("o_ps", [128, 2, CH], F32))
        u_mm, u_done, o_mm, r_done, out_done = (sem("mlp_" + n) for n in ("u_mm", "u_done", "o_mm", "r_done", "out_done"))
        stored = [sem(f"mlp_stored{i}") for i in range(4)]
        block = ctx.enter_context(nc.Block())
        NC = B * CPB

        @block.tensor
        def _(pe):
            for n in range(NC + 1):
                if n < NC:
                    if n >= 2:
                        pe.wait_ge(u_done, n - 1)
                    nc.tensor.matmul(PU[:, n % 2, :], G[:, n // CPB, :], X[:, n * CH:(n + 1) * CH], start=True, stop=True).then_inc(u_mm, 1)
                if n >= 1:
                    pe.wait_ge(u_done, n)
                    if n >= 3:
                        pe.wait_ge(r_done, n - 2)
                    nc.tensor.matmul(PO[:, (n - 1) % 2, :], o2[:], U[:, (n - 1) % 2, :], start=True, stop=True).then_inc(o_mm, 1)

        @block.scalar
        def _(act):
            for n in range(NC + 2):
                if n < NC:
                    act.wait_ge(u_mm, n + 1)
                    if n >= 2:
                        act.wait_ge(o_mm, n - 1)
                    nc.scalar.activation(U[:, n % 2, :], PU[:, n % 2, :], ACT.Gelu).then_inc(u_done, 1)
                if n >= 2:
                    k = n - 2
                    act.wait_ge(r_done, k + 1)
                    if k >= 4:
                        act.wait_ge(stored[k % 4], 16 * (k // 4))
                    nc.scalar.activation(O[:, k % 4, :], R[:, k % 2, :], ACT.Gelu).then_inc(out_done, 1)

        @block.vector
        def _(dve):
            for n in range(NC):
                dve.wait_ge(o_mm, n + 1)
                if n >= 2:
                    dve.wait_ge(out_done, n - 1)
                nc.vector.tensor_tensor(R[:, n % 2, :], PO[:, n % 2, :], X[:, n * CH:(n + 1) * CH], ALU.add).then_inc(r_done, 1)

        @block.sync
        def _(sp):
            for n in range(NC):
                sp.wait_ge(out_done, n + 1)
                sp.dma_start(out[:, n // CPB, (n % CPB) * CH:(n % CPB + 1) * CH], O[:, n % 4, :]).then_inc(stored[n % 4], 16)
            for i in range(4):
                sp.wait_ge(stored[i], 16 * (NC // 4))


class Kept:
    pass


def program(nc, d, out):
    with ExitStack() as ctx:
        X = ctx.enter_context(nc.sbuf_tensor("x_all", [128, N], F32))
        with ExitStack() as l0:
            sb = lambda n, s, dt=F32: l0.enter_context(nc.sbuf_tensor(n, s, dt))
            t = Kept()
            t.qk_w = sb("qk_w", [128, HEADS, 2, 96])
            t.qk_full = sb("qk_full", [128, 256])
            t.v_w = sb("v_w", [128, 128])
            t.proj_w = sb("proj_w", [128, 128])
            t.qk_b = sb("qk_b", [96, 2 * HEADS])
            t.ident = sb("ident", [128, 128])
            t.ident16 = sb("ident16", [128, 128], F16)
            t.sel = sb("sel", [97, 2, HD])
            t.ones = sb("ones_sq", [128, HD])
            t.qk_scale = sb("qk_scale", [128, 4])
            t.out_b = sb("out_b", [128, 1])
            setup_attention(nc, d, X, t)
            attention(nc, X, t)
        binary_conv(nc, d, X)
        mamba(nc, d, X)
        linear_attention(nc, d, X, out)


def more_arrays(arrays, g, col, np):
    w1 = g("L1_conv_w")
    arrays["l1_wt"] = w1.transpose(1, 2, 3, 0).reshape(C, TAPS * C)
    arrays["l1_wr"] = w1.reshape(C, C * TAPS)
    arrays["l1_vec"] = np.concatenate([col(g("L1_conv_" + n)) for n in ("bias0", "gamma", "beta", "bias1", "alpha", "bias2")], axis=1)
    two = lambda a: np.reshape(a, (DH, 128, -1)).transpose(1, 0, 2)
    wx = g("L2_conv_W_x")
    arrays["l2_w_in"] = g("L2_conv_W_in")
    arrays["l2_w_out"] = two(g("L2_conv_W_out"))
    arrays["l2_w_bcr"] = np.concatenate([np.tile(two(wx[:, DTR:]), (1, 1, 3)), two(wx[:, :DTR])], axis=2)
    arrays["l2_w_dt"] = np.concatenate([np.zeros((BCR, DI), np.float32), g("L2_conv_dt_w")])
    arrays["l2_alog"] = two(g("L2_conv_A_log")).reshape(128, DH * NS)
    halves = lambda n: two(g("L2_conv_" + n)).reshape(128, -1)
    b_in = np.reshape(g("L2_conv_b_in"), (4, 128)).T
    arrays["l2_vec"] = np.concatenate([col(g("L2_conv_b_out")), col(g("L2_conv_b_out")), halves("conv_b"), halves("dt_b"), halves("D"), b_in,
                                       col(g("L2_conv_ln_g")), col(g("L2_conv_ln_b")), halves("conv_w")], axis=1)
    arrays["l2_onehot"] = np.tile(np.eye(2 * NS, dtype=np.float32), (3, 1))
    w3 = np.reshape(g("L3_conv_qkv_w"), (H3, 3, HC3, C))
    arrays["l3_qw"] = w3[:, 0].reshape(C, C)
    arrays["l3_kvw"] = w3[:, 1:3].transpose(3, 1, 0, 2).reshape(C, 2 * C)
    arrays["l3_o1"] = g("L3_conv_o1_w").T
    arrays["l3_o2"] = g("L3_conv_o2_w").T
    for n in "wb":
        kn, vn = g("L3_conv_kln_" + n), g("L3_conv_vln_" + n)
        arrays["l3_ln" + n] = np.tile(np.concatenate([np.reshape(kn, (1, C)), np.reshape(vn, (1, C))], axis=1), (128, 1))
    arrays["l3_mask"] = np.kron(np.eye(H3), np.full((HC3, HC3), 1.0 / HW)).astype(np.float32)


def kernel(**inputs):
    import numpy as np
    import concourse.bacc as bacc
    from concourse.bass_utils import run_bass_kernel_spmd

    g = lambda n: np.asarray(inputs[n])
    col = lambda a: np.reshape(a, (-1, 1))
    arrays = {}
    arrays["x"] = np.reshape(g("x"), (B, C, HW)).transpose(1, 0, 2)
    w, wb = g("L0_conv_qkv_w"), g("L0_conv_qkv_b")
    wq = np.reshape(w[:2 * C], (2, HEADS, HD, C)).transpose(3, 1, 0, 2)
    arrays["qk_w"] = np.tile(wq[:, :, :, None, :], (1, 1, 1, 3, 1)).reshape(C, HEADS, 2, 3 * HD)
    bq = np.reshape(wb[:2 * C], (2, HEADS, HD)).transpose(2, 1, 0)
    arrays["qk_b"] = np.tile(bq[None], (3, 1, 1, 1)).reshape(3 * HD, 2 * HEADS)
    arrays["qk_full"] = w[:2 * C].T
    arrays["v_w"] = w[2 * C:].T
    arrays["proj_w"] = g("L0_conv_proj_w").T
    arrays["l0_vec"] = np.concatenate([col(g("L0_conv_gn_w")), col(g("L0_conv_gn_b")), col(wb[2 * C:]), col(g("L0_conv_proj_b")),
                                       col(wb[:C]), col(wb[C:2 * C]), col(wb[:C]), col(wb[:C])], axis=1)
    cg = C // GROUPS
    arrays["group_avg"] = np.kron(np.eye(GROUPS), np.full((cg, cg), 1.0 / cg)).astype(np.float32)
    arrays["ones_row"] = np.ones((1, 128), np.float32)
    arrays["ones"] = np.ones((128, HD), np.float32)
    arrays["ident"] = np.eye(128, dtype=np.float32)
    sel = np.zeros((97, 2, HD), np.float32)
    for half in (0, 64):
        sel[half:half + HD, 0, :] = np.eye(HD)
        sel[half + HD, 1, :] = 1.0
    arrays["sel"] = sel
    more_arrays(arrays, g, col, np)

    nc = bacc.Bacc("TRN2", target_bir_lowering=False, num_devices=1)
    d = {}
    for name in arrays:
        arrays[name] = np.ascontiguousarray(arrays[name])
        d[name] = nc.dram_tensor("in_" + name, arrays[name].shape, mybir.dt.from_np(arrays[name].dtype), kind="ExternalInput").ap()
    out = nc.dram_tensor("out", (B, C, HW), F32, kind="ExternalOutput").ap()
    program(nc, d, out.rearrange("b c n -> c b n"))
    r = run_bass_kernel_spmd(nc, [{"in_" + k: v for k, v in arrays.items()}], core_ids=[0])
    return np.reshape(r.results[0]["out"], (B, C, H, W))
```
